# Optimizing a Trainium2 kernel written in Bass

```python
import numpy as np
import jax
import jax.numpy as jnp

def _softmax(x, axis=-1):
    return jax.nn.softmax(x, axis=axis)
def _gelu(x):
    return jax.nn.gelu(x, approximate=True)
def _silu(x):
    return jax.nn.silu(x)
def _sigmoid(x):
    return jax.nn.sigmoid(x)
def _layernorm(x, axis=-1, eps=1e-5):
    m = jnp.mean(x, axis=axis, keepdims=True)
    v = jnp.var(x, axis=axis, keepdims=True)
    return (x - m) / jnp.sqrt(v + eps)
def _scatter_add(tgt, idx, src, axis=0):
    return tgt.at[idx].add(src)
def _segment_sum(src, seg, n):
    return jax.ops.segment_sum(src, seg, n)

kernel_name = 'mk_metaformer_d1_conv_nchw128_2e225b'

def setup_inputs(seed: int = 0):
    np.random.seed(seed)
    _w = jnp.asarray
    def _rec_inputs():
        import jax
        import jax.numpy as jnp
        _gk = jax.random.key(seed)
        x = -8.268e-05 + 0.9999 * jax.random.normal(jax.random.fold_in(_gk, 1), (128, 128, 56, 56), jnp.float32)
        return x
    x = _rec_inputs()
    def _L0_conv_setup():
        import jax, jax.numpy as jnp
        import numpy as np
        SHIFT = 1
        key = jax.random.key(seed)
        kx, kw = jax.random.split(key)
        x = jax.random.normal(kx, (128, 128, 56, 56), dtype=jnp.float32)
        W = jax.random.normal(kw, (32, 3, 2, 3, 4), dtype=jnp.float32)
        return {'x': x, 'W': W}
    _L0_conv_all = _L0_conv_setup()
    _L0_conv_in = {k: v for k, v in _L0_conv_all.items() if k in ('W', )}
    del _L0_conv_all

    def _L0_ffn_setup():
        import jax, jax.numpy as jnp
        import numpy as np
        BN_EPS = 1e-05
        key = jax.random.key(seed)
        k1, k2, k3 = jax.random.split(key, 3)
        B, T, I, H = (64, 2048, 128, 128)
        x = jax.random.normal(k1, (B, T, I), dtype=jnp.float32)
        W = jax.random.normal(k2, (H, I), dtype=jnp.float32) * (1.0 / np.sqrt(I))
        V = jnp.linalg.qr(jax.random.normal(k3, (H, H), dtype=jnp.float32))[0]
        gamma = jnp.ones((H,), dtype=jnp.float32)
        beta = jnp.zeros((H,), dtype=jnp.float32)
        return {'x': x, 'W': W, 'V': V, 'gamma': gamma, 'beta': beta}
    _L0_ffn_all = _L0_ffn_setup()
    _L0_ffn_in = {k: v for k, v in _L0_ffn_all.items() if k in ('W', 'V', 'gamma', 'beta', )}
    del _L0_ffn_all

    return {
        "x": x,
        "L0_conv_W": _L0_conv_in["W"],
        "L0_ffn_W": _L0_ffn_in["W"],
        "L0_ffn_V": _L0_ffn_in["V"],
        "L0_ffn_gamma": _L0_ffn_in["gamma"],
        "L0_ffn_beta": _L0_ffn_in["beta"],
    }

def reference(x, L0_conv_W, L0_ffn_W, L0_ffn_V, L0_ffn_gamma, L0_ffn_beta):
    import jax
    import jax.numpy as jnp
    def _L0_conv_ref(x, W):
        import jax, jax.numpy as jnp
        import numpy as np
        SHIFT = 1
        n = x.shape[0]
        t = x.reshape(n, 2, 64, 56, 56).sum(axis=1)
        t = t.reshape(n, 32, 2, 56, 56)
        tp = jnp.pad(t, ((0, 0), (1, 1), (0, 0), (0, 0), (0, 0)))
        w1 = jnp.stack([tp[:, i:i + 32] for i in range(3)], axis=1)
        w1 = jnp.roll(w1, SHIFT, axis=5)
        wp = jnp.pad(w1, ((0, 0), (0, 0), (0, 0), (0, 0), (0, 0), (1, 1)))
        w2 = jnp.stack([wp[..., l:l + 56] for l in range(3)], axis=5)
        out = jnp.einsum('nijmplo,jimlk->njpok', w2, W)
        t5 = out.transpose(0, 2, 3, 1, 4).reshape(n, 56, 56, 128)
        t5 = jnp.roll(t5, SHIFT, axis=1)
        return t5.transpose(0, 3, 1, 2)

    def _L0_ffn_ref(x, W, V, gamma, beta):
        import jax, jax.numpy as jnp
        import numpy as np
        BN_EPS = 1e-05
        B, T, H = (x.shape[0], x.shape[1], W.shape[0])
        Wx = jnp.einsum('bti,hi->bth', x, W)
        flat = Wx.reshape(B * T, H)
        mean = jnp.mean(flat, axis=0)
        var = jnp.var(flat, axis=0)
        Wx = ((flat - mean) * jax.lax.rsqrt(var + BN_EPS) * gamma + beta).reshape(B, T, H)
        Vt = V.T

        def step(yt, wx_t):
            yt = jax.nn.sigmoid(wx_t + yt @ Vt)
            return (yt, yt)
        y0 = jnp.zeros((B, H), dtype=Wx.dtype)
        _, ys = jax.lax.scan(step, y0, jnp.swapaxes(Wx, 0, 1))
        return jnp.swapaxes(ys, 0, 1)

    def _gn(v, G=32, eps=1e-5):
        B_, C_, H_, W_ = v.shape
        g = v.reshape(B_, G, C_ // G, H_, W_)
        m = jnp.mean(g, axis=(2, 3, 4), keepdims=True)
        s = jnp.var(g, axis=(2, 3, 4), keepdims=True)
        return ((g - m) / jnp.sqrt(s + eps)).reshape(v.shape)

    def _ln_c(v, eps=1e-6):
        m = jnp.mean(v, axis=1, keepdims=True)
        s = jnp.var(v, axis=1, keepdims=True)
        return (v - m) / jnp.sqrt(s + eps)

    def _ln_t(v, eps=1e-5):
        m = jnp.mean(v, axis=-1, keepdims=True)
        s = jnp.var(v, axis=-1, keepdims=True)
        return (v - m) / jnp.sqrt(s + eps)

    def _to_tokens(v):
        B_, C_, H_, W_ = v.shape
        return v.reshape(B_, C_, H_ * W_).transpose(0, 2, 1)
    def _from_tokens(t, like):
        B_, C_, H_, W_ = like.shape
        return t.transpose(0, 2, 1).reshape(B_, C_, H_, W_)

    x = x + _L0_conv_ref(_ln_c(x), L0_conv_W)
    t = _to_tokens(x)
    t = t + _L0_ffn_ref(_ln_t(t), L0_ffn_W, L0_ffn_V, L0_ffn_gamma, L0_ffn_beta)
    x = _from_tokens(t, x)
    return x


_drawn_inputs = setup_inputs


def setup_inputs(seed=0):
    import zlib

    import numpy as np

    out = dict(_drawn_inputs(seed))
    spreads = {'L0_ffn_gamma': (1.0, 0.6), 'L0_ffn_beta': (0.0, 2.0)}
    factors = {'L0_ffn_V': 3.155}
    for name, (base, spread) in spreads.items():
        noise = np.random.default_rng([zlib.crc32(name.encode()), seed]).standard_normal(out[name].shape)
        drawn = base * np.exp(spread * noise) if base else spread * noise
        out[name] = jnp.asarray(drawn.astype(out[name].dtype))
    for name, factor in factors.items():
        out[name] = (out[name] * factor).astype(out[name].dtype)
    return out
```

```python
from contextlib import ExitStack

import concourse.bass as bass
from concourse import mybir

ALU = mybir.AluOpType
ACT = mybir.ActivationFunctionType
F32 = mybir.dt.float32
BF16 = mybir.dt.bfloat16

B, C, H, W = 128, 128, 56, 56
TOK = H * W
HALF = C // 2
TAPS = 3
ROWS = 8
TN = ROWS * W
TPI = TOK // TN
TILES = B * TPI
SLOTS = 4
TURN = SLOTS * TPI
TURNS = TILES // TURN
PADW = W + 2
EPS_C, EPS_T, EPS_BN = 1e-6, 1e-5, 1e-5

LAG_NORM = 11
LAG_WRAP = 12
LAG_CONV = 13
LAG_SUMS1 = 14
LAG_U = 25
LAG_Z = 26
LAST = 27
NORMS = B + LAG_SUMS1 // TPI

CH = 112
CHUNKS = TOK // CH
RING = 3
GRP = 28
BT = 4
BLOCKS = TOK // BT
BPG = GRP // BT
BPC = CH // BT
PAIR = 2 * BPG


def at_least(eng, sem, value):
    if not isinstance(value, int) or value > 0:
        eng.wait_ge(sem, value)


def own_instruction(eng, sem):
    eng.sem_inc(sem, 1)


class Tile:

    def __init__(self, turn, base, j, lag):
        self.n = base + (j - lag)
        self.live = not isinstance(turn, int) or 0 <= self.n < TILES
        at = (j - lag) % TURN
        self.turn = turn if j >= lag else turn - 1
        self.at = at
        self.slot = at // TPI
        self.g = at % TPI
        self.image = self.turn * SLOTS + self.slot


def ticks(eng, tick):
    for j in range(TURN):
        tick(0, 0, j)
    with eng.Fori(1, TURNS) as turn:
        base = eng.snap(turn * TURN)
        for j in range(TURN):
            tick(turn, base, j)
    for j in range(LAST):
        tick(TURNS, TILES, j)


def metaformer_layer(nc, x, conv_w, ffn_w, ffn_v, gamma, beta, out):
    x1_dram = nc.dram_tensor("x1_dram", (CHUNKS, C, B, CH), F32).ap()
    rstd_dram = nc.dram_tensor("rstd_dram", (3, B, TOK), BF16).ap()
    x_tok = x.rearrange("b c h w -> b c (h w)")
    out_tok = out.rearrange("b c h w -> c b (h w)")

    with ExitStack() as ctx:
        def sb(name, shape, dt=F32):
            return ctx.enter_context(nc.sbuf_tensor(name, shape, dt))

        def sem(name):
            return ctx.enter_context(nc.semaphore(name))

        arena = sb("arena", [128, RING * B * CH])
        taken = [0]

        def carve(size):
            a = arena[:, taken[0]:taken[0] + size]
            taken[0] += size
            return a

        xs = carve(SLOTS * TOK).rearrange("p (s h w) -> p s h w", s=SLOTS, w=W)
        x1s = carve(2 * TOK).rearrange("p (s t) -> p s t", s=2)
        xsq = carve(2 * TN).rearrange("p (s t) -> p s t", s=2)
        x1sq = carve(2 * TN).rearrange("p (s t) -> p s t", s=2)
        xn = carve(4 * ROWS * PADW).rearrange("p (s r w) -> p s r w", s=4, w=PADW)
        us = carve(2 * TN).rearrange("p (s t) -> p s t", s=2)
        zstat = carve(TURN * 6).rearrange("p (n k) -> p n k", k=6)
        zturn = carve(TURNS * 3).rearrange("p (n k) -> p n k", k=3)
        msq = carve(TN)
        var = carve(TN)
        sd = carve(TN)
        rs = carve(TN)
        nt = carve(TN)
        rn = carve(TN)
        rd = carve(TN)
        chunk = arena[:, :].rearrange("p (s t) -> p s t", t=CH)

        part = [sb(f"part{i}", [64, TN], BF16) for i in range(3)]
        r3a = [sb(f"r3a{i}", [96, TN], BF16) for i in range(2)]
        r3b = [sb(f"r3b{i}", [96, TN], BF16) for i in range(2)]
        cw = sb("cw", [128, TAPS, 128])
        center = sb("center", [128, 128])
        ident = sb("ident", [128, 128])
        w_nat = sb("w_nat", [128, 128])
        w_t = sb("w_t", [128, 128])
        wc_nat = sb("wc_nat", [128, 128])
        wc_t = sb("wc_t", [128, 128])
        v_nat = sb("v_nat", [128, 128])
        v_t = sb("v_t", [128, 128])
        a_t = sb("a_t", [128, 128])
        pick = sb("pick", [96, TPI, 128], BF16)
        row_mean = sb("row_mean", [128, 63])
        ones3 = sb("ones3", [3, 512], BF16)
        gam = sb("gam", [128, 1])
        bet = sb("bet", [128, 1])
        epsc = sb("epsc", [64, 1])
        vec = sb("vec", [128, 16])
        b3f = sb("b3f", [128, 3])
        b3b = sb("b3b", [128, 3], BF16)
        b3t = sb("b3t", [3, 128], BF16)
        zmv = sb("zmv", [128, 2])
        rg = [sb(f"rg{i}", [3, B, GRP], BF16) for i in range(2)]
        xr = [sb(f"xr{i}", [128, BT, B]) for i in range(2)]
        ys = [sb(f"ys{i}", [128, BT, B]) for i in range(2)]

        banks = [ctx.enter_context(nc.psum_tensor(f"bank{i}", [128, 512], F32)) for i in range(8)]
        sums = banks[0:2]
        rbank, ubank = banks[2], banks[3]
        cbank, zbank = banks[4:6], banks[6:8]
        rcbank, pre = banks[0:2], banks[2:4]

        s_param = sem("param_loaded")
        s_band = sem("band_loaded")
        s_zero = sem("zeroed")
        s_const = sem("center_ready")
        s_fixed = sem("fixed_values_ready")
        s_prep = sem("prep_product")
        s_prepc = sem("prep_copied")
        s_wready = sem("weights_ready")
        s_x = [sem(f"x_loaded{i}") for i in range(SLOTS)]
        s_sq = sem("square_ready")
        s_sum0 = sem("tile_summed")
        s_msq = sem("mean_squared")
        s_sub = sem("variance_raw")
        s_var = sem("variance_ready")
        s_sd = sem("deviation_ready")
        s_rec = sem("reciprocal_ready")
        s_pool = sem("pool_step")
        s_parts = sem("rstd_parts_ready")
        s_r3 = sem("rstd_rows_ready")
        s_rb = sem("rstd_spread")
        s_xn = sem("normed_ready")
        s_wrap = sem("wrapped_ready")
        s_conv = sem("conv_ready")
        s_x1 = sem("x1_ready")
        s_sq1 = sem("x1_square_ready")
        s_sum1 = sem("x1_tile_summed")
        s_ru = sem("rstd1_spread")
        s_u = sem("u_ready")
        s_z = sem("z_ready")
        s_bn = sem("z_stats_ready")
        s_agg = sem("turn_stats_ready")
        s_x1st = [sem(f"x1_stored{i}") for i in range(2)]
        s_rst = [sem(f"rstd_stored{i}") for i in range(2)]
        s_bnv = sem("bn_step")
        s_bnp = sem("bn_product")
        s_bsd = sem("bn_deviation")
        s_bnok = sem("bn_weights_ready")
        s_passa = sem("pass_a_over")
        s_tally = sem("waits_over")
        s_ch = [sem(f"chunk_loaded{i}") for i in range(RING)]
        s_rg = [sem(f"group_loaded{i}") for i in range(2)]
        s_rc = sem("rstd_block_spread")
        s_xr = sem("scaled_block_ready")
        s_inj = sem("block_projected")
        s_pre = sem("preactivation_ready")
        s_y = sem("state_ready")
        s_out = sem("block_added")
        s_st = sem("chunk_stored")

        block = ctx.enter_context(nc.Block())

        @block.sync
        def _(sp):
            sp.dma_start(w_nat[:, :], ffn_w).then_inc(s_param, 16)
            sp.dma_start(v_nat[:, :], ffn_v).then_inc(s_param, 16)
            sp.dma_start(gam[:, :], gamma.rearrange("(h o) -> h o", o=1)).then_inc(s_param, 16)
            sp.dma_start(bet[:, :], beta.rearrange("(h o) -> h o", o=1)).then_inc(s_param, 16)
            for p in range(SLOTS):
                sp.dma_start(xs[:, p].rearrange("p h w -> p (h w)"), x_tok[p]).then_inc(s_x[p], 16)
            sp.wait_ge(s_zero, 1)
            for j in range(HALF // 2):
                i0, i1 = max(0, 1 - j), min(TAPS, HALF // 2 + 1 - j)
                for top in (0, HALF):
                    row = top + 2 * (j + i0 - 1)
                    sp.dma_start(cw[row:row + 2 * (i1 - i0), :, 4 * j:4 * j + 4],
                                 conv_w[j, i0:i1].rearrange("i m l k -> (i m) l k")).then_inc(s_band, 16)

            def image(turn, at, last):
                done = turn * SLOTS + at + 1
                sp.wait_ge(s_x1, done * TPI)
                if not last:
                    sp.dma_start(xs[:, at].rearrange("p h w -> p (h w)"),
                                 x_tok[done + (SLOTS - 1)]).then_inc(s_x[at], 16)
                at_image = bass.ds(done - 1, 1)
                sp.dma_start(x1_dram[:, :, at_image, :].rearrange("k c o t -> c (k o) t"),
                             x1s[:, at % 2].rearrange("p (k t) -> p k t", t=CH)).then_inc(s_x1st[at % 2], 16)
                sp.wait_ge(s_r3, done + LAG_SUMS1 // TPI)
                for q in range(3):
                    sp.dma_start(rstd_dram[q, at_image, :].rearrange("o (g t) -> (o g) t", g=TPI),
                                 r3b[at % 2][32 * q:32 * q + TPI, :]).then_inc(s_rst[at % 2], 16)

            with sp.Fori(0, TURNS - 1) as turn:
                for at in range(SLOTS):
                    image(turn, at, False)
            for at in range(SLOTS):
                image(TURNS - 1, at, True)

            for i in range(2):
                sp.wait_ge(s_x1st[i], 16 * B // 2)
                sp.wait_ge(s_rst[i], 48 * B // 2)
            sp.wait_ge(s_passa, 1)

            def load_group(parity, first):
                sp.dma_start(rg[parity][:, :, :], rstd_dram[:, :, bass.ds(first, GRP)]).then_inc(s_rg[parity], 16)

            load_group(0, 0)
            load_group(1, GRP)
            for c in range(RING):
                sp.dma_start(chunk[:, c * B:(c + 1) * B, :], x1_dram[c]).then_inc(s_ch[c], 16)

            def chunk_step(c, slot, n_groups, store_before, load):
                if store_before:
                    prev = (slot + RING - 1) % RING
                    sp.wait_ge(s_out, c * BPC)
                    sp.dma_start(out_tok[:, :, bass.ds((c - 1) * CH, CH)],
                                 chunk[:, prev * B:(prev + 1) * B, :]).then_inc(s_st, 16)
                for q in range(n_groups):
                    sp.wait_ge(s_rc, (c * (BPC // BPG) + (q + 1)) * BPG)
                    load_group(q % 2, (c * (BPC // BPG) + q + 2) * GRP)
                    if q == 0 and load:
                        sp.wait_ge(s_st, c * 16)
                        sp.dma_start(chunk[:, prev * B:(prev + 1) * B, :],
                                     x1_dram[bass.ds(c + (RING - 1), 1)].rearrange("o c b t -> (o c) b t")
                                     ).then_inc(s_ch[prev], 16)

            G = BPC // BPG
            chunk_step(0, 0, G, False, False)
            with sp.Fori(0, (CHUNKS - 1 - RING) // RING) as lap:
                for k in range(1, RING + 1):
                    chunk_step(lap * RING + k, k % RING, G, True, True)
            first = 1 + (CHUNKS - 1 - RING) // RING * RING
            for c in range(first, CHUNKS):
                chunk_step(c, c % RING, G if c < CHUNKS - 1 else G - 2, True, c + RING - 1 < CHUNKS)
            sp.wait_ge(s_out, BLOCKS)
            slot = (CHUNKS - 1) % RING
            sp.dma_start(out_tok[:, :, TOK - CH:TOK], chunk[:, slot * B:(slot + 1) * B, :]).then_inc(s_st, 16)
            sp.wait_ge(s_st, 16 * CHUNKS)

        @block.gpsimd
        def _(pool):
            pool.memset(cw[:, :, :], 0.0).then_inc(s_zero, 1)
            pool.memset(ident[:, :], 0.0).then_inc(s_zero, 1)
            pool.memset(pick[:, :, :], 0.0).then_inc(s_zero, 1)
            pool.wait_ge(s_zero, 3)
            pool.affine_select(out=ident[:, :], in_=ident[:, :], compare_op=ALU.not_equal, fill=1.0, base=0,
                               pattern=[[-1, 128]], channel_multiplier=1).then_inc(s_zero, 1)
            for q in range(3):
                pool.wait_ge(s_zero, 4 + q)
                v = pick[32 * q:32 * q + 32, :, :]
                pool.affine_select(out=v, in_=v, compare_op=ALU.not_equal, fill=1.0, base=0,
                                   pattern=[[-1, TPI], [0, 128]], channel_multiplier=1).then_inc(s_zero, 1)
            pool.wait_ge(s_zero, 7)
            pool.tensor_scalar(center[:, :], ident[:, :], -1.0 / C, None, ALU.add).then_inc(s_const, 1)

            with pool.Fori(0, NORMS) as r:
                step = pool.snap(r * 8)

                def then(k, ins):
                    ins.then_inc(s_pool, 1)
                    pool.wait_ge(s_pool, step + (k + 1))
                    own_instruction(pool, s_tally)

                pool.wait_ge(s_rec, r + 1)
                then(0, pool.tensor_tensor(nt[0:64, :], rs[0:64, :], rs[0:64, :], ALU.mult))
                then(1, pool.tensor_tensor(nt[0:64, :], nt[0:64, :], var[0:64, :], ALU.mult))
                then(2, pool.tensor_scalar(nt[0:64, :], nt[0:64, :], -0.5, 1.5, ALU.mult, ALU.add))
                then(3, pool.tensor_tensor(rn[0:64, :], rs[0:64, :], nt[0:64, :], ALU.mult))
                then(4, pool.tensor_copy(part[0][:, :], rn[0:64, :]))
                then(5, pool.tensor_tensor(rd[0:64, :], rn[0:64, :], part[0][:, :], ALU.subtract))
                then(6, pool.tensor_copy(part[1][:, :], rd[0:64, :]))
                then(7, pool.tensor_tensor(part[2][:, :], rd[0:64, :], part[1][:, :], ALU.subtract))
                pool.sem_inc(s_parts, 1)

            with pool.Fori(0, CHUNKS) as c:
                slot = pool.snap((c % RING) * B)
                with pool.Fori(0, BPC // 2) as m2:
                    for k in range(2):
                        m = m2 * 2 + k
                        n = c * BPC + m
                        pool.wait_ge(s_y, (n + 1) * BT)
                        v = chunk[:, bass.ds(slot, B), bass.ds(m * BT, BT)]
                        pool.tensor_tensor(v, v, ys[k][:, :, :].rearrange("p t b -> p b t"),
                                           ALU.add).then_inc(s_out, 1)

        @block.scalar
        def _(act):
            def tick(turn, base, j):
                t = Tile(turn, base, j, 0)
                n_norm = turn * SLOTS + j // TPI
                norm = j % TPI == 0 and (not isinstance(turn, int) or 0 < n_norm <= NORMS)
                if norm:
                    if not isinstance(turn, int) or n_norm <= B:
                        act.wait_ge(s_sum0, n_norm * TPI)
                    at_least(act, s_sum1, n_norm * TPI - LAG_SUMS1)
                    act.activation(msq[0:64, :], sums[(n_norm_parity(j))][0:64, 0:TN], ACT.Square).then_inc(s_msq, 1)
                if t.live:
                    if t.g == 0:
                        act.wait_ge(s_x[t.slot], 16 * (t.turn + 1))
                    at_least(act, s_sum0, t.n - 1)
                    act.activation(xsq[:, t.at % 2], xs[:, t.slot, ROWS * t.g:ROWS * (t.g + 1), :],
                                   ACT.Square).then_inc(s_sq, 1)
                t = Tile(turn, base, j, LAG_WRAP)
                if t.live:
                    act.wait_ge(s_xn, t.n + 1)
                    act.copy(xn[:, t.at % 4, :, 1:2], xn[:, t.at % 4, :, PADW - 1:PADW]).then_inc(s_wrap, 1)
                t = Tile(turn, base, j, LAG_SUMS1)
                if t.live:
                    act.wait_ge(s_x1, t.n + 1)
                    at_least(act, s_sum1, t.n - 1)
                    act.activation(x1sq[:, t.at % 2], x1s[:, t.slot % 2, TN * t.g:TN * (t.g + 1)],
                                   ACT.Square).then_inc(s_sq1, 1)
                if norm:
                    act.wait_ge(s_var, n_norm)
                    act.activation(sd[0:64, :], var[0:64, :], ACT.Sqrt).then_inc(s_sd, 1)

            ticks(act, tick)
            act.wait_ge(s_bnv, 2)
            act.activation(vec[:, 1:2], vec[:, 0:1], ACT.Sqrt).then_inc(s_bsd, 1)

            def two_blocks(n0, at0):
                for k in range(2):
                    at_least(act, s_out, n0 + (k - 1))
                    for t in range(BT):
                        act.wait_ge(s_pre, at0 + (BT * k + t + 1))
                        act.activation(ys[k][:, t, :], pre[k][:, B * t:B * (t + 1)], ACT.Sigmoid).then_inc(s_y, 1)

            two_blocks(0, 0)
            with act.Fori(2, BLOCKS, 2) as n0:
                two_blocks(n0, act.snap(n0 * BT))

        @block.vector
        def _(dve):
            dve.memset(sums[0][:, :], 0.0).then_inc(s_fixed, 1)
            dve.memset(sums[1][:, :], 0.0).then_inc(s_fixed, 1)
            dve.memset(row_mean[:, :], 0.0).then_inc(s_fixed, 1)
            dve.memset(ones3[:, :], 1.0).then_inc(s_fixed, 1)
            dve.memset(xn[:, :, :, 0:1], 0.0).then_inc(s_fixed, 1)
            dve.memset(zturn[:, :, 0:1], 1.0).then_inc(s_fixed, 1)
            dve.memset(epsc[0:32, :], EPS_C).then_inc(s_fixed, 1)
            dve.memset(epsc[32:64, :], EPS_T).then_inc(s_fixed, 1)
            dve.memset(ys[1][:, BT - 1, :], 0.0).then_inc(s_fixed, 1)
            dve.wait_ge(s_fixed, 9)
            dve.memset(row_mean[:, 31:32], 1.0 / C).then_inc(s_fixed, 1)
            copies = [(w_t[:, :], 0, 128), (v_t[:, :], 1, 128), (wc_t[:, :], 2, 128), (wc_nat[:, :], 3, 128)]
            for k, (dst, b, n) in enumerate(copies):
                dve.wait_ge(s_prep, k + 1)
                dve.tensor_copy(dst, banks[2 + b][:, 0:n]).then_inc(s_prepc, 1)
            dve.wait_ge(s_prep, 5)
            dve.tensor_copy(cw[:, :, :].rearrange("p l k -> p (l k)"),
                            banks[6][:, 0:TAPS * 128]).then_inc(s_prepc, 1)

            def tick(turn, base, j):
                n_norm = turn * SLOTS + j // TPI
                norm = not isinstance(turn, int) or 0 < n_norm <= NORMS
                if norm and j % TPI == 0:
                    dve.wait_ge(s_msq, n_norm)
                    dve.tensor_tensor(var[0:64, :], sums[n_norm_parity(j)][64:128, 0:TN], msq[0:64, :],
                                      ALU.subtract).then_inc(s_sub, 1)
                    dve.wait_ge(s_sub, n_norm)
                    dve.tensor_scalar(var[0:64, :], var[0:64, :], 0.0, epsc[:, 0:1],
                                      ALU.max, ALU.add).then_inc(s_var, 1)
                if norm and j % TPI == 1:
                    dve.wait_ge(s_sd, n_norm)
                    dve.reciprocal(rs[0:64, :], sd[0:64, :]).then_inc(s_rec, 1)
                if norm and j % TPI == 3:
                    dve.wait_ge(s_parts, n_norm)
                    first = Tile(turn, base, j - 3 - TPI, 0)
                    second = Tile(turn, base, j - 3 - TPI - LAG_SUMS1, 0)
                    par = n_norm_parity(j - 3)
                    if second.live and (not isinstance(turn, int) or second.n >= 2 * TPI):
                        dve.wait_ge(s_rst[par], 48 * (second.turn * 2 + second.slot // 2))
                    for q in range(3):
                        if first.live:
                            last = dve.tensor_copy(r3a[par][32 * q:32 * q + 32, :], part[q][0:32, :])
                        if second.live:
                            last = dve.tensor_copy(r3b[par][32 * q:32 * q + 32, :], part[q][32:64, :])
                    last.then_inc(s_r3, 1)
                t = Tile(turn, base, j, LAG_NORM)
                if t.live:
                    dve.wait_ge(s_rb, t.n + 1)
                    at_least(dve, s_conv, t.n - 3)
                    rb = rbank[:, 0:TN].rearrange("p (r w) -> p r w", w=W)
                    r0 = ROWS * t.g - 1
                    dst = xn[:, t.at % 4, :, 2:PADW]
                    if t.g == 0:
                        dve.tensor_tensor(dst[:, 0:1, :], xs[:, t.slot, H - 1:H, :], rb[:, 0:1, :], ALU.mult)
                        last = dve.tensor_tensor(dst[:, 1:ROWS, :], xs[:, t.slot, 0:ROWS - 1, :], rb[:, 1:ROWS, :],
                                                 ALU.mult)
                    else:
                        last = dve.tensor_tensor(dst, xs[:, t.slot, r0:r0 + ROWS, :], rb, ALU.mult)
                    last.then_inc(s_xn, 1)
                t = Tile(turn, base, j, LAG_CONV)
                if t.live:
                    dve.wait_ge(s_conv, t.n + 1)
                    if t.g == 0 and (not isinstance(turn, int) or t.n >= 2 * TPI):
                        dve.wait_ge(s_x1st[t.slot % 2], 16 * (t.turn * 2 + t.slot // 2))
                    dve.tensor_tensor(x1s[:, t.slot % 2, TN * t.g:TN * (t.g + 1)],
                                      xs[:, t.slot, ROWS * t.g:ROWS * (t.g + 1), :].rearrange("p h w -> p (h w)"),
                                      cbank[t.at % 2][:, 0:TN], ALU.add).then_inc(s_x1, 1)
                t = Tile(turn, base, j, LAG_U)
                if t.live:
                    dve.wait_ge(s_ru, t.n + 1)
                    at_least(dve, s_z, t.n - 1)
                    dve.tensor_tensor(us[:, t.at % 2], x1s[:, t.slot % 2, TN * t.g:TN * (t.g + 1)], ubank[:, 0:TN],
                                      ALU.mult).then_inc(s_u, 1)
                t = Tile(turn, base, j, LAG_Z)
                if t.live:
                    dve.wait_ge(s_z, t.n + 1)
                    dve.bn_stats(zstat[:, t.at, :], zbank[t.at % 2][:, 0:TN]).then_inc(s_bn, 1)
                    if t.at == TURN - 1:
                        dve.wait_ge(s_bn, t.n + 1)
                        own_instruction(dve, s_tally)
                        dve.bn_aggr(zmv[:, :], zstat[:, :, :].rearrange("p n k -> p (n k)")).then_inc(s_agg, 1)
                        dve.wait_ge(s_agg, 2 * t.turn + 1)
                        dst = zturn[:, bass.ds(t.turn, 1), 1:3].rearrange("p o k -> p (o k)")
                        dve.tensor_copy(dst, zmv[:, :]).then_inc(s_agg, 1)

            ticks(dve, tick)

            count = [0]

            def step(ins):
                count[0] += 1
                ins.then_inc(s_bnv, 1)
                dve.wait_ge(s_bnv, count[0])

            def v(i):
                return vec[:, i:i + 1]

            dve.wait_ge(s_agg, 2 * TURNS)
            step(dve.bn_aggr(zmv[:, :], zturn[:, :, :].rearrange("p n k -> p (n k)")))
            step(dve.tensor_scalar(v(0), zmv[:, 1:2], EPS_BN, None, ALU.add))
            dve.sem_inc(s_passa, 1)
            dve.wait_ge(s_bsd, 1)
            step(dve.reciprocal(v(2), v(1)))
            step(dve.tensor_tensor(v(3), v(2), v(2), ALU.mult))
            step(dve.tensor_tensor(v(3), v(3), v(0), ALU.mult))
            step(dve.tensor_scalar(v(3), v(3), -0.5, 1.5, ALU.mult, ALU.add))
            step(dve.tensor_tensor(v(4), v(2), v(3), ALU.mult))
            dve.wait_ge(s_param, 64)
            step(dve.tensor_tensor(v(5), v(4), gam[:, :], ALU.mult))
            step(dve.tensor_tensor(v(6), v(5), zmv[:, 0:1], ALU.mult))
            step(dve.tensor_tensor(v(7), bet[:, :], v(6), ALU.subtract))
            step(dve.tensor_scalar(w_t[:, :], ident[:, :], v(5), None, ALU.mult))
            step(dve.tensor_copy(b3b[:, 0:1], v(7)))
            step(dve.tensor_copy(b3f[:, 0:1], b3b[:, 0:1]))
            step(dve.tensor_tensor(v(8), v(7), b3f[:, 0:1], ALU.subtract))
            step(dve.tensor_copy(b3b[:, 1:2], v(8)))
            step(dve.tensor_copy(b3f[:, 1:2], b3b[:, 1:2]))
            step(dve.tensor_tensor(v(9), v(8), b3f[:, 1:2], ALU.subtract))
            step(dve.tensor_copy(b3b[:, 2:3], v(9)))
            step(dve.tensor_copy(b3f[:, 2:3], b3b[:, 2:3]))
            dve.sem_inc(s_bnok, 1)
            dve.wait_ge(s_bnp, 2)
            dve.tensor_copy(a_t[:, :], banks[4][:, 0:128]).then_inc(s_bnok, 1)
            dve.tensor_copy(b3t[:, :], banks[5][0:3, 0:128]).then_inc(s_bnok, 1)

            def scale(m, k, slot, n):
                dve.wait_ge(s_rc, n + 1)
                at_least(dve, s_inj, n - 1)
                dve.tensor_tensor(xr[k][:, :, :].rearrange("p t b -> p b t"),
                                  chunk[:, slot * B:(slot + 1) * B, bass.ds(m * BT, BT)],
                                  rcbank[k][:, :].rearrange("p (b t) -> p b t", t=BT), ALU.mult).then_inc(s_xr, 1)

            dve.wait_ge(s_ch[0], 16)
            for k in range(2):
                scale(k, k, 0, k)
            with dve.Fori(1, BPC // 2) as m:
                for k in range(2):
                    scale(m * 2 + k, k, 0, m * 2 + k)
            with dve.Fori(0, (CHUNKS - 1) // RING) as lap:
                for r in range(1, RING + 1):
                    slot = r % RING
                    dve.wait_ge(s_ch[slot], 16 * (lap + r // RING + 1))
                    own_instruction(dve, s_tally)
                    first = dve.snap((lap * RING + r) * BPC)
                    with dve.Fori(0, BPC // 2) as m:
                        for k in range(2):
                            scale(m * 2 + k, k, slot, first + (m * 2 + k))

        @block.tensor
        def _(pe):
            pe.wait_ge(s_param, 64)
            pe.wait_ge(s_const, 1)
            pe.wait_ge(s_fixed, 10)
            pe.transpose(banks[2][:, 0:128], w_nat[:, :], ident[:, :]).then_inc(s_prep, 1)
            pe.transpose(banks[3][:, 0:128], v_nat[:, :], ident[:, :]).then_inc(s_prep, 1)
            pe.wait_ge(s_prepc, 1)
            pe.matmul(banks[4][:, 0:128], center[:, :], w_t[:, :], start=True, stop=True).then_inc(s_prep, 1)
            pe.matmul(banks[5][:, 0:128], w_t[:, :], center[:, :], start=True, stop=True).then_inc(s_prep, 1)
            pe.wait_ge(s_band, 16 * HALF)
            pe.matmul(banks[6][:, 0:TAPS * 128], center[:, :], cw[:, :, :].rearrange("p l k -> p (l k)"),
                      start=True, stop=True).then_inc(s_prep, 1)
            pe.wait_ge(s_prepc, 5)

            def tick(turn, base, j):
                t = Tile(turn, base, j, LAG_NORM)
                if t.live:
                    if t.g == 0:
                        pe.wait_ge(s_r3, t.image + 1)
                    at_least(pe, s_xn, t.n)
                    par = t.slot % 2
                    pe.matmul(rbank[:, 0:W], pick[:, (t.g - 1) % TPI, :], r3a[par][:, TN - W:TN],
                              start=True, stop=True)
                    pe.matmul(rbank[:, W:TN], pick[:, t.g, :], r3a[par][:, 0:TN - W],
                              start=True, stop=True).then_inc(s_rb, 1)
                t = Tile(turn, base, j, LAG_CONV)
                if t.live:
                    pe.wait_ge(s_wrap, t.n + 1)
                    at_least(pe, s_x1, t.n - 1)
                    o, v = cbank[t.at % 2], xn[:, t.at % 4]
                    pe.matmul(o[:, 0:TN], cw[:, 1, :], v[:, :, 1:W + 1], start=True, stop=False)
                    pe.matmul(o[:, 0:TN], cw[:, 0, :], v[:, :, 0:W], start=False, stop=False)
                    pe.matmul(o[:, 0:TN].rearrange("p (r w) -> p r w", w=W)[:, :, 0:W - 1], cw[:, 2, :],
                              v[:, :, 2:W + 1], start=False, stop=True).then_inc(s_conv, 1)
                t = Tile(turn, base, j, LAG_U)
                if t.live:
                    if t.g == 0:
                        pe.wait_ge(s_r3, t.image + (1 + LAG_SUMS1 // TPI))
                    at_least(pe, s_u, t.n)
                    pe.matmul(ubank[:, 0:TN], pick[:, t.g, :], r3b[t.slot % 2][:, :],
                              start=True, stop=True).then_inc(s_ru, 1)
                t = Tile(turn, base, j, LAG_Z)
                if t.live:
                    pe.wait_ge(s_u, t.n + 1)
                    at_least(pe, s_bn, t.n - 1)
                    pe.matmul(zbank[t.at % 2][:, 0:TN], wc_t[:, :], us[:, t.at % 2], start=True,
                              stop=True).then_inc(s_z, 1)
                t, t1 = Tile(turn, base, j, 0), Tile(turn, base, j, LAG_SUMS1)
                sel = row_mean[:, 31 - j % TPI:63 - j % TPI]
                first, last = j % TPI == 0, j % TPI == TPI - 1
                bank = sums[t.slot % 2]
                if (t.live or t1.live) and first:
                    at_least(pe, s_sub, turn * SLOTS + j // TPI - 1)
                if t.live:
                    if first:
                        pe.wait_ge(s_x[t.slot], 16 * (t.turn + 1))
                    pe.matmul(bank[0:32, 0:TN], sel,
                              xs[:, t.slot, ROWS * t.g:ROWS * (t.g + 1), :].rearrange("p h w -> p (h w)"),
                              start=first, stop=last)
                    pe.wait_ge(s_sq, t.n + 1)
                    pe.matmul(bank[64:96, 0:TN], sel, xsq[:, t.at % 2], start=first, stop=last).then_inc(s_sum0, 1)
                if t1.live:
                    pe.wait_ge(s_sq1, t1.n + 1)
                    pe.matmul(bank[32:64, 0:TN], sel, x1s[:, t1.slot % 2, TN * t1.g:TN * (t1.g + 1)],
                              start=first, stop=last)
                    pe.matmul(bank[96:128, 0:TN], sel, x1sq[:, t1.at % 2], start=first,
                              stop=last).then_inc(s_sum1, 1)

            ticks(pe, tick)

            pe.wait_ge(s_bnok, 1)
            pe.matmul(banks[4][:, 0:128], wc_nat[:, :], w_t[:, :], start=True, stop=True).then_inc(s_bnp, 1)
            pe.transpose(banks[5][0:3, 0:128], b3f[:, :], ident[:, :]).then_inc(s_bnp, 1)
            pe.wait_ge(s_bnok, 3)

            def spread(n, k, g):
                at_least(pe, s_xr, n - 1)
                parity, first = g
                pe.matmul(rcbank[k][:, :], ones3[:, 0:128], rg[parity][:, :, BT * first:BT * (first + 1)],
                          start=True, stop=True).then_inc(s_rc, 1)

            def offset(k):
                pe.matmul(pre[k][:, :], b3t[:, :], ones3[:, :], start=True, stop=False, skip_group_check=True)

            def project(k, t):
                ins = pe.matmul(pre[k][:, B * t:B * (t + 1)], a_t[:, :], xr[k][:, t, :], start=False,
                                stop=False, skip_group_check=True)
                if t == BT - 1:
                    ins.then_inc(s_inj, 1)

            def recur(k, t):
                y = ys[k][:, t - 1, :] if t else ys[1 - k][:, BT - 1, :]
                pe.matmul(pre[k][:, B * t:B * (t + 1)], v_t[:, :], y, start=False, stop=True,
                          skip_group_check=True).then_inc(s_pre, 1)

            def group_of(i):
                return i // BPG % 2, i % BPG

            pe.wait_ge(s_rg[0], 16)
            spread(0, 0, group_of(0))
            spread(1, 1, group_of(1))
            offset(0)
            pe.wait_ge(s_xr, 1)
            for t in range(BT):
                project(0, t)

            def turn_of_blocks(q, base, last):
                for i in range(PAIR):
                    n = base + i
                    k = i % 2
                    for t in range(BT):
                        at_least(pe, s_y, n * BT + t)
                        recur(k, t)
                        if t == 1 and not (last and i + 2 >= PAIR):
                            if (i + 2) % BPG == 0:
                                pe.wait_ge(s_rg[(i + 2) // BPG % 2], (q + (2 if i + 2 == PAIR else 1)) * 16)
                            spread(n + 2, k, group_of(i + 2))
                        if not (last and i + 1 >= PAIR):
                            if t == 0:
                                offset(1 - k)
                                pe.wait_ge(s_xr, n + 2)
                            project(1 - k, t)

            turn_of_blocks(0, 0, False)
            with pe.Fori(1, BLOCKS // PAIR - 1) as q:
                turn_of_blocks(q, pe.snap(q * PAIR), False)
            turn_of_blocks(BLOCKS // PAIR - 1, BLOCKS - PAIR, True)


def n_norm_parity(j):
    return (j // TPI - 1) % 2


_INS = ['x', 'L0_conv_W', 'L0_ffn_W', 'L0_ffn_V', 'L0_ffn_gamma', 'L0_ffn_beta']


def kernel(**inputs):
    import numpy as np
    import concourse.bacc as bacc
    from concourse.bass_utils import run_bass_kernel_spmd

    nc = bacc.Bacc("TRN2", target_bir_lowering=False, num_devices=1)
    arrays, args = {}, []
    for name in _INS:
        a = np.ascontiguousarray(inputs[name])
        arrays[f"in_{name}"] = a
        args.append(nc.dram_tensor(f"in_{name}", a.shape, mybir.dt.from_np(a.dtype), kind="ExternalInput").ap())
    out = nc.dram_tensor("out_x", (B, C, H, W), F32, kind="ExternalOutput").ap()
    metaformer_layer(nc, *args, out)
    r = run_bass_kernel_spmd(nc, [arrays], core_ids=[0])
    return r.results[0]["out_x"]
```

```python
from contextlib import ExitStack

import concourse.bass as bass
from concourse import mybir

ALU = mybir.AluOpType
ACT = mybir.ActivationFunctionType
F32 = mybir.dt.float32
BF16 = mybir.dt.bfloat16
F16 = mybir.dt.float16

B, C, H, W = 128, 128, 56, 56
TOK = H * W
HALF = C // 2
TAPS = 3
ROWS = 8
TN = ROWS * W
TPI = TOK // TN
TILES = B * TPI
SLOTS = 4
TURN = SLOTS * TPI
TURNS = TILES // TURN
PADW = W + 2
EPS_C, EPS_T, EPS_BN = 1e-6, 1e-5, 1e-5

LAG_NORM = 11
LAG_HIGH = 11
LAG_LOW = 12
LAG_CONV = 13
LAG_SUMS1 = 14
LAG_U = 25
LAG_UHIGH = 25
LAG_ULOW = 26
LAG_Z = 27
LAST = 27
FILL = 2
NSTEPS = 7
NORMS = B + LAG_SUMS1 // TPI

CH = 112
CHUNKS = TOK // CH
RING = 3
GRP = 28
BT = 4
BLOCKS = TOK // BT
BPG = GRP // BT
BPC = CH // BT
PAIR = 2 * BPG


def at_least(eng, sem, value):
    if not isinstance(value, int) or value > 0:
        eng.wait_ge(sem, value)


def own_instruction(eng, sem):
    eng.sem_inc(sem, 1)


class Tile:

    def __init__(self, turn, base, j, lag):
        self.n = base + (j - lag)
        self.live = not isinstance(turn, int) or 0 <= self.n < TILES
        at = (j - lag) % TURN
        self.turn = turn if j >= lag else turn - 1
        self.at = at
        self.slot = at // TPI
        self.g = at % TPI
        self.image = self.turn * SLOTS + self.slot


def ticks(eng, tick):
    for j in range(FILL * TURN):
        tick(j // TURN, j // TURN * TURN, j % TURN)
    with eng.Fori(FILL, TURNS) as turn:
        base = eng.snap(turn * TURN)
        for j in range(TURN):
            tick(turn, base, j)
    for j in range(LAST):
        tick(TURNS, TILES, j)


def metaformer_layer(nc, x, conv_w, ffn_w, ffn_v, gamma, beta, out):
    x1_dram = nc.dram_tensor("x1_dram", (CHUNKS, C, B, CH), F32).ap()
    rstd_dram = nc.dram_tensor("rstd_dram", (3, B, TOK), BF16).ap()
    x_tok = x.rearrange("b c h w -> b c (h w)")
    out_tok = out.rearrange("b c h w -> c b (h w)")

    with ExitStack() as ctx:
        def sb(name, shape, dt=F32):
            return ctx.enter_context(nc.sbuf_tensor(name, shape, dt))

        def sem(name):
            return ctx.enter_context(nc.semaphore(name))

        arena = sb("arena", [128, RING * B * CH])
        taken = [0]

        def carve(size):
            a = arena[:, taken[0]:taken[0] + size]
            taken[0] += size
            return a

        xs = carve(SLOTS * TOK).rearrange("p (s h w) -> p s h w", s=SLOTS, w=W)
        x1s = carve(2 * TOK).rearrange("p (s t) -> p s t", s=2)
        xsq = carve(2 * TN).rearrange("p (s t) -> p s t", s=2)
        x1sq = carve(2 * TN).rearrange("p (s t) -> p s t", s=2)
        xn = carve(4 * ROWS * PADW).rearrange("p (s r w) -> p s r w", s=4, w=PADW)
        us = carve(4 * TN).rearrange("p (s t) -> p s t", s=4)
        zstat = carve(TURN * 6).rearrange("p (n k) -> p n k", k=6)
        zturn = carve(TURNS * 3).rearrange("p (n k) -> p n k", k=3)
        msq = carve(TN)
        var = carve(TN)
        ln = carve(TN)
        rs = carve(TN)
        nt = carve(TN)
        rd = carve(TN)

        def halves(size):
            return carve(size // 2).bitcast(F16)

        xh = halves(4 * ROWS * PADW).rearrange("p (s r w) -> p s r w", s=4, w=PADW)
        xl = halves(4 * ROWS * PADW).rearrange("p (s r w) -> p s r w", s=4, w=PADW)
        uh = halves(4 * TN).rearrange("p (s t) -> p s t", s=4)
        ul = halves(4 * TN).rearrange("p (s t) -> p s t", s=4)
        chunk = arena[:, :].rearrange("p (s t) -> p s t", t=CH)

        part = [sb(f"part{i}", [64, TN], BF16) for i in range(3)]
        r3a = [sb(f"r3a{i}", [96, TN], BF16) for i in range(2)]
        r3b = [sb(f"r3b{i}", [96, TN], BF16) for i in range(2)]
        cw = sb("cw", [128, TAPS, 128])
        cw_h = sb("cw_h", [128, TAPS, 128], F16)
        cw_l = sb("cw_l", [128, TAPS, 128], F16)
        wc_h = sb("wc_h", [128, 128], F16)
        wc_l = sb("wc_l", [128, 128], F16)
        center = sb("center", [128, 128])
        ident = sb("ident", [128, 128])
        w_nat = sb("w_nat", [128, 128])
        w_t = sb("w_t", [128, 128])
        wc_nat = sb("wc_nat", [128, 128])
        v_nat = sb("v_nat", [128, 128])
        v_t = sb("v_t", [128, 128])
        a_t = sb("a_t", [128, 128])
        pick = sb("pick", [96, TPI, 128], BF16)
        row_mean = sb("row_mean", [128, 63])
        ones3 = sb("ones3", [3, 512], BF16)
        gam = sb("gam", [128, 1])
        bet = sb("bet", [128, 1])
        epsc = sb("epsc", [64, 1])
        vec = sb("vec", [128, 16])
        b3f = sb("b3f", [128, 3])
        b3b = sb("b3b", [128, 3], BF16)
        b3t = sb("b3t", [3, 128], BF16)
        zmv = sb("zmv", [128, 2])
        rg = [sb(f"rg{i}", [3, B, GRP], BF16) for i in range(2)]
        xr = [sb(f"xr{i}", [128, BT, B]) for i in range(2)]
        ys = [sb(f"ys{i}", [128, BT, B]) for i in range(2)]

        banks = [ctx.enter_context(nc.psum_tensor(f"bank{i}", [128, 512], F32)) for i in range(8)]
        sums = banks[0:2]
        rbank, ubank = banks[2], banks[3]
        cbank, zbank = banks[4:6], banks[6:8]
        rcbank, pre = banks[0:2], banks[2:4]

        s_param = sem("param_loaded")
        s_band = sem("band_loaded")
        s_zero = sem("zeroed")
        s_const = sem("center_ready")
        s_fixed = sem("fixed_values_ready")
        s_prep = sem("prep_product")
        s_prepc = sem("prep_copied")
        s_wready = sem("weights_ready")
        s_x = [sem(f"x_loaded{i}") for i in range(SLOTS)]
        s_sq = sem("square_ready")
        s_sum0 = sem("tile_summed")
        s_msq = sem("mean_squared")
        s_sub = sem("variance_raw")
        s_var = sem("variance_ready")
        s_ln = sem("log_variance_ready")
        s_est = sem("rstd_estimated")
        s_norm = sem("rstd_step")
        s_r3a = sem("rstd_rows_ready")
        s_r3b = sem("rstd1_rows_ready")
        s_rb = sem("rstd_spread")
        s_xn = sem("normed_ready")
        s_wrap = sem("wrapped_ready")
        s_xh = sem("normed_high_ready")
        s_xl = sem("normed_low_ready")
        s_conv = sem("conv_ready")
        s_x1 = sem("x1_ready")
        s_sq1 = sem("x1_square_ready")
        s_sum1 = sem("x1_tile_summed")
        s_ru = sem("rstd1_spread")
        s_u = sem("u_ready")
        s_uh = sem("u_high_ready")
        s_ul = sem("u_low_ready")
        s_z = sem("z_ready")
        s_bn = sem("z_stats_ready")
        s_agg = sem("turn_stats_ready")
        s_x1st = [sem(f"x1_stored{i}") for i in range(2)]
        s_rst = [sem(f"rstd_stored{i}") for i in range(2)]
        s_bnv = sem("bn_step")
        s_bnp = sem("bn_product")
        s_bsd = sem("bn_deviation")
        s_bnok = sem("bn_weights_ready")
        s_passa = sem("pass_a_over")
        s_tally = sem("waits_over")
        s_ch = [sem(f"chunk_loaded{i}") for i in range(RING)]
        s_rg = [sem(f"group_loaded{i}") for i in range(2)]
        s_rc = sem("rstd_block_spread")
        s_xr = sem("scaled_block_ready")
        s_inj = sem("block_projected")
        s_pre = sem("preactivation_ready")
        s_y = sem("state_ready")
        s_out = sem("block_added")
        s_st = [sem(f"chunk_part_stored{i}") for i in range(4)]

        block = ctx.enter_context(nc.Block())

        @block.sync
        def _(sp):
            sp.dma_start(w_nat[:, :], ffn_w).then_inc(s_param, 16)
            sp.dma_start(v_nat[:, :], ffn_v).then_inc(s_param, 16)
            sp.dma_start(gam[:, :], gamma.rearrange("(h o) -> h o", o=1)).then_inc(s_param, 16)
            sp.dma_start(bet[:, :], beta.rearrange("(h o) -> h o", o=1)).then_inc(s_param, 16)
            for p in range(SLOTS):
                sp.dma_start(xs[:, p].rearrange("p h w -> p (h w)"), x_tok[p]).then_inc(s_x[p], 16)
            sp.wait_ge(s_zero, 1)
            for j in range(HALF // 2):
                i0, i1 = max(0, 1 - j), min(TAPS, HALF // 2 + 1 - j)
                for top in (0, HALF):
                    row = top + 2 * (j + i0 - 1)
                    sp.dma_start(cw[row:row + 2 * (i1 - i0), :, 4 * j:4 * j + 4],
                                 conv_w[j, i0:i1].rearrange("i m l k -> (i m) l k")).then_inc(s_band, 16)

            def image(turn, at, last):
                done = turn * SLOTS + at + 1
                sp.wait_ge(s_x1, done * TPI)
                if not last:
                    sp.dma_start(xs[:, at].rearrange("p h w -> p (h w)"),
                                 x_tok[done + (SLOTS - 1)]).then_inc(s_x[at], 16)
                at_image = bass.ds(done - 1, 1)
                sp.dma_start(x1_dram[:, :, at_image, :].rearrange("k c o t -> c (k o) t"),
                             x1s[:, at % 2].rearrange("p (k t) -> p k t", t=CH)).then_inc(s_x1st[at % 2], 16)
                sp.wait_ge(s_r3b, done)
                for q in range(3):
                    sp.dma_start(rstd_dram[q, at_image, :].rearrange("o (g t) -> (o g) t", g=TPI),
                                 r3b[at % 2][32 * q:32 * q + TPI, :]).then_inc(s_rst[at % 2], 16)

            with sp.Fori(0, TURNS - 1) as turn:
                for at in range(SLOTS):
                    image(turn, at, False)
            for at in range(SLOTS):
                image(TURNS - 1, at, True)

            for i in range(2):
                sp.wait_ge(s_x1st[i], 16 * B // 2)
                sp.wait_ge(s_rst[i], 48 * B // 2)
            sp.wait_ge(s_passa, 1)

            def load_group(parity, first):
                sp.dma_start(rg[parity][:, :, :], rstd_dram[:, :, bass.ds(first, GRP)]).then_inc(s_rg[parity], 16)

            QB = B // 4

            def load_part(c, slot, q):
                at = slot * B + q * QB
                sp.dma_start(chunk[:, at:at + QB, :],
                             x1_dram[bass.ds(c, 1), :, q * QB:(q + 1) * QB, :].rearrange("o c b t -> (o c) b t")
                             ).then_inc(s_ch[slot], 16)

            def store_part(c, slot, q):
                at = slot * B + q * QB
                sp.dma_start(out_tok[:, q * QB:(q + 1) * QB, bass.ds(c * CH, CH)],
                             chunk[:, at:at + QB, :]).then_inc(s_st[q], 16)

            load_group(0, 0)
            for q in range(4):
                load_part(0, 0, q)
            load_group(1, GRP)
            for c in range(1, RING):
                for q in range(4):
                    load_part(c, c, q)

            G = BPC // BPG

            def chunk_step(c, slot, groups, store, load):
                prev = (slot + RING - 1) % RING
                for q in range(G):
                    if q < groups:
                        sp.wait_ge(s_rc, (c * G + (q + 1)) * BPG)
                        load_group(q % 2, (c * G + (q + 2)) * GRP)
                    if store:
                        if q == 0:
                            sp.wait_ge(s_out, c * BPC)
                        store_part(c - 1, prev, q)
                    if load and q > 0:
                        sp.wait_ge(s_st[q - 1], c * 16)
                        load_part(c + (RING - 1), prev, q - 1)
                if load:
                    sp.wait_ge(s_st[G - 1], c * 16)
                    load_part(c + (RING - 1), prev, G - 1)

            chunk_step(0, 0, G, False, False)
            with sp.Fori(0, (CHUNKS - 1 - RING) // RING) as lap:
                for k in range(1, RING + 1):
                    chunk_step(lap * RING + k, k % RING, G, True, True)
            first = 1 + (CHUNKS - 1 - RING) // RING * RING
            for c in range(first, CHUNKS):
                chunk_step(c, c % RING, G if c < CHUNKS - 1 else G - 2, True, c + RING - 1 < CHUNKS)
            sp.wait_ge(s_out, BLOCKS)
            for q in range(4):
                store_part(CHUNKS - 1, (CHUNKS - 1) % RING, q)
            for q in range(4):
                sp.wait_ge(s_st[q], 16 * CHUNKS)

        @block.gpsimd
        def _(pool):
            pool.memset(cw[:, :, :], 0.0).then_inc(s_zero, 1)
            pool.memset(ident[:, :], 0.0).then_inc(s_zero, 1)
            pool.memset(pick[:, :, :], 0.0).then_inc(s_zero, 1)
            pool.wait_ge(s_zero, 3)
            pool.affine_select(out=ident[:, :], in_=ident[:, :], compare_op=ALU.not_equal, fill=1.0, base=0,
                               pattern=[[-1, 128]], channel_multiplier=1).then_inc(s_zero, 1)
            for q in range(3):
                pool.wait_ge(s_zero, 4 + q)
                v = pick[32 * q:32 * q + 32, :, :]
                pool.affine_select(out=v, in_=v, compare_op=ALU.not_equal, fill=1.0, base=0,
                                   pattern=[[-1, TPI], [0, 128]], channel_multiplier=1).then_inc(s_zero, 1)
            pool.wait_ge(s_zero, 7)
            pool.tensor_scalar(center[:, :], ident[:, :], -1.0 / C, None, ALU.add).then_inc(s_const, 1)

            def tick(turn, base, j):
                t = Tile(turn, base, j, LAG_LOW)
                if t.live:
                    pool.wait_ge(s_xh, t.n + 1)
                    at_least(pool, s_conv, t.n - 3)
                    pool.tensor_tensor(xl[:, t.at % 4, :, 1:PADW], xn[:, t.at % 4, :, 1:PADW],
                                       xh[:, t.at % 4, :, 1:PADW], ALU.subtract).then_inc(s_xl, 1)
                t = Tile(turn, base, j, LAG_ULOW)
                if t.live:
                    pool.wait_ge(s_uh, t.n + 1)
                    at_least(pool, s_z, t.n - 3)
                    pool.tensor_tensor(ul[:, t.at % 4], us[:, t.at % 4], uh[:, t.at % 4],
                                       ALU.subtract).then_inc(s_ul, 1)

            ticks(pool, tick)

            with pool.Fori(0, CHUNKS) as c:
                slot = pool.snap((c % RING) * B)
                with pool.Fori(0, BPC // 2) as m2:
                    for k in range(2):
                        m = m2 * 2 + k
                        n = c * BPC + m
                        pool.wait_ge(s_y, (n + 1) * BT)
                        v = chunk[:, bass.ds(slot, B), bass.ds(m * BT, BT)]
                        pool.tensor_tensor(v, v, ys[k][:, :, :].rearrange("p t b -> p b t"),
                                           ALU.add).then_inc(s_out, 1)

        @block.scalar
        def _(act):
            def tick(turn, base, j):
                t = Tile(turn, base, j, 0)
                n_norm = turn * SLOTS + j // TPI
                norm = j % TPI == 0 and (not isinstance(turn, int) or 0 < n_norm <= NORMS)
                if norm:
                    if not isinstance(turn, int) or n_norm <= B:
                        act.wait_ge(s_sum0, n_norm * TPI)
                    at_least(act, s_sum1, n_norm * TPI - LAG_SUMS1)
                    act.activation(msq[0:64, :], sums[(n_norm_parity(j))][0:64, 0:TN], ACT.Square).then_inc(s_msq, 1)
                if t.live:
                    if t.g == 0:
                        act.wait_ge(s_x[t.slot], 16 * (t.turn + 1))
                    at_least(act, s_sum0, t.n - 1)
                    act.activation(xsq[:, t.at % 2], xs[:, t.slot, ROWS * t.g:ROWS * (t.g + 1), :],
                                   ACT.Square).then_inc(s_sq, 1)
                t = Tile(turn, base, j, LAG_SUMS1)
                if t.live:
                    act.wait_ge(s_x1, t.n + 1)
                    at_least(act, s_sum1, t.n - 1)
                    act.activation(x1sq[:, t.at % 2], x1s[:, t.slot % 2, TN * t.g:TN * (t.g + 1)],
                                   ACT.Square).then_inc(s_sq1, 1)
                w = Tile(turn, base, j, LAG_HIGH)
                if w.live:
                    act.wait_ge(s_xn, w.n + 1)
                    act.copy(xn[:, w.at % 4, :, 1:2], xn[:, w.at % 4, :, PADW - 1:PADW]).then_inc(s_wrap, 1)
                if norm:
                    act.wait_ge(s_var, n_norm)
                    act.activation(ln[0:64, :], var[0:64, :], ACT.Ln).then_inc(s_ln, 1)
                if w.live:
                    act.wait_ge(s_wrap, w.n + 1)
                    at_least(act, s_conv, w.n - 3)
                    act.copy(xh[:, w.at % 4, :, 1:PADW], xn[:, w.at % 4, :, 1:PADW]).then_inc(s_xh, 1)
                if norm:
                    act.wait_ge(s_ln, n_norm)
                    act.activation(rs[0:64, :], ln[0:64, :], ACT.Exp, scale=-0.5).then_inc(s_est, 1)
                t = Tile(turn, base, j, LAG_UHIGH)
                if t.live:
                    act.wait_ge(s_u, t.n + 1)
                    at_least(act, s_z, t.n - 3)
                    act.copy(uh[:, t.at % 4], us[:, t.at % 4]).then_inc(s_uh, 1)

            act.preload_act_table_set("natural_log_exp_and_others")
            ticks(act, tick)
            act.wait_ge(s_bnv, 2)
            act.activation(vec[:, 1:2], vec[:, 0:1], ACT.Sqrt).then_inc(s_bsd, 1)

            def two_blocks(n0, at0):
                for k in range(2):
                    at_least(act, s_out, n0 + (k - 1))
                    for t in range(BT):
                        act.wait_ge(s_pre, at0 + (BT * k + t + 1))
                        act.activation(ys[k][:, t, :], pre[k][:, B * t:B * (t + 1)], ACT.Sigmoid).then_inc(s_y, 1)

            two_blocks(0, 0)
            with act.Fori(2, BLOCKS, 2) as n0:
                two_blocks(n0, act.snap(n0 * BT))

        @block.vector
        def _(dve):
            dve.memset(sums[0][:, :], 0.0).then_inc(s_fixed, 1)
            dve.memset(sums[1][:, :], 0.0).then_inc(s_fixed, 1)
            dve.memset(row_mean[:, :], 0.0).then_inc(s_fixed, 1)
            dve.memset(ones3[:, :], 1.0).then_inc(s_fixed, 1)
            dve.memset(xh[:, :, :, 0:1], 0.0).then_inc(s_fixed, 1)
            dve.memset(xl[:, :, :, 0:1], 0.0).then_inc(s_fixed, 1)
            dve.memset(zturn[:, :, 0:1], 1.0).then_inc(s_fixed, 1)
            dve.memset(epsc[0:32, :], EPS_C).then_inc(s_fixed, 1)
            dve.memset(epsc[32:64, :], EPS_T).then_inc(s_fixed, 1)
            dve.memset(ys[1][:, BT - 1, :], 0.0).then_inc(s_fixed, 1)
            dve.wait_ge(s_fixed, 10)
            dve.memset(row_mean[:, 31:32], 1.0 / C).then_inc(s_fixed, 1)
            for k, (dst, bank) in enumerate([(w_t, banks[2]), (v_t, banks[3]), (None, None), (wc_nat, banks[5])]):
                dve.wait_ge(s_prep, k + 1)
                if dst is not None:
                    dve.tensor_copy(dst[:, :], bank[:, 0:128]).then_inc(s_prepc, 1)
            dve.tensor_copy(wc_h[:, :], banks[4][:, 0:128]).then_inc(s_prepc, 1)
            dve.wait_ge(s_prepc, 4)
            dve.tensor_tensor(wc_l[:, :], banks[4][:, 0:128], wc_h[:, :], ALU.subtract).then_inc(s_prepc, 1)

            def band_parts():
                flat = banks[6][:, 0:TAPS * 128]
                high, low = (a[:, :, :].rearrange("p l k -> p (l k)") for a in (cw_h, cw_l))
                dve.wait_ge(s_prep, 5)
                dve.tensor_copy(high, flat).then_inc(s_prepc, 1)
                dve.wait_ge(s_prepc, 6)
                dve.tensor_tensor(low, flat, high, ALU.subtract).then_inc(s_prepc, 1)

            def norm_step(turn, base, j, gap):
                n_norm = turn * SLOTS + j // TPI
                if isinstance(turn, int) and not 0 < n_norm <= NORMS:
                    return
                at = (j % TPI, gap)
                r, q, d = rs[0:64, :], nt[0:64, :], rd[0:64, :]
                before = (n_norm - 1) * NSTEPS

                def then(k, needed, ins):
                    if needed:
                        dve.wait_ge(s_norm, before + k)
                    ins().then_inc(s_norm, 1)

                if at == (0, 0):
                    dve.wait_ge(s_msq, n_norm)
                    dve.tensor_tensor(var[0:64, :], sums[n_norm_parity(j)][64:128, 0:TN], msq[0:64, :],
                                      ALU.subtract).then_inc(s_sub, 1)
                elif at == (0, 1):
                    dve.wait_ge(s_sub, n_norm)
                    dve.tensor_scalar(var[0:64, :], var[0:64, :], 0.0, epsc[:, 0:1],
                                      ALU.max, ALU.add).then_inc(s_var, 1)
                elif at == (1, 1):
                    dve.wait_ge(s_est, n_norm)
                    then(0, False, lambda: dve.scalar_tensor_tensor(out=q, in0=r, scalar=-0.5, in1=r,
                                                                    op0=ALU.mult, op1=ALU.mult))
                elif at == (1, 2):
                    then(1, True, lambda: dve.tensor_tensor(q, q, var[0:64, :], ALU.mult))
                elif at == (2, 0):
                    then(2, True, lambda: dve.scalar_tensor_tensor(out=q, in0=q, scalar=1.5, in1=r,
                                                                   op0=ALU.add, op1=ALU.mult))
                elif at == (2, 1):
                    then(3, True, lambda: dve.tensor_copy(part[0][:, :], q))
                elif at == (2, 2):
                    then(4, True, lambda: dve.tensor_tensor(d, q, part[0][:, :], ALU.subtract))
                elif at == (3, 0):
                    then(5, True, lambda: dve.tensor_copy(part[1][:, :], d))
                elif at == (3, 1):
                    then(6, True, lambda: dve.tensor_tensor(part[2][:, :], d, part[1][:, :], ALU.subtract))
                elif at == (3, 2):
                    dve.wait_ge(s_norm, before + NSTEPS)
                    if Tile(turn, base, j - 3 - TPI, 0).live:
                        for k in range(3):
                            last = dve.tensor_copy(r3a[n_norm_parity(j - 3)][32 * k:32 * k + 32, :], part[k][0:32, :])
                        last.then_inc(s_r3a, 1)
                elif at == (4, 0):
                    second = Tile(turn, base, j - 4 - TPI - LAG_SUMS1, 0)
                    par = n_norm_parity(j - 4)
                    if second.live:
                        if not isinstance(turn, int) or second.n >= 2 * TPI:
                            dve.wait_ge(s_rst[par], 48 * (second.turn * 2 + second.slot // 2))
                        for k in range(3):
                            last = dve.tensor_copy(r3b[par][32 * k:32 * k + 32, :], part[k][32:64, :])
                        last.then_inc(s_r3b, 1)

            def tick(turn, base, j):
                if isinstance(turn, int) and turn == 0 and j == LAG_NORM - 1:
                    band_parts()
                norm_step(turn, base, j, 0)
                t = Tile(turn, base, j, LAG_NORM)
                if t.live:
                    dve.wait_ge(s_rb, t.n + 1)
                    at_least(dve, s_xl, t.n - 3)
                    rb = rbank[:, 0:TN].rearrange("p (r w) -> p r w", w=W)
                    r0 = ROWS * t.g - 1
                    dst = xn[:, t.at % 4, :, 2:PADW]
                    if t.g == 0:
                        dve.tensor_tensor(dst[:, 0:1, :], xs[:, t.slot, H - 1:H, :], rb[:, 0:1, :], ALU.mult)
                        last = dve.tensor_tensor(dst[:, 1:ROWS, :], xs[:, t.slot, 0:ROWS - 1, :], rb[:, 1:ROWS, :],
                                                 ALU.mult)
                    else:
                        last = dve.tensor_tensor(dst, xs[:, t.slot, r0:r0 + ROWS, :], rb, ALU.mult)
                    last.then_inc(s_xn, 1)
                norm_step(turn, base, j, 1)
                t = Tile(turn, base, j, LAG_CONV)
                if t.live:
                    dve.wait_ge(s_conv, t.n + 1)
                    if t.g == 0 and (not isinstance(turn, int) or t.n >= 2 * TPI):
                        dve.wait_ge(s_x1st[t.slot % 2], 16 * (t.turn * 2 + t.slot // 2))
                    dve.tensor_tensor(x1s[:, t.slot % 2, TN * t.g:TN * (t.g + 1)],
                                      xs[:, t.slot, ROWS * t.g:ROWS * (t.g + 1), :].rearrange("p h w -> p (h w)"),
                                      cbank[t.at % 2][:, 0:TN], ALU.add).then_inc(s_x1, 1)
                norm_step(turn, base, j, 2)
                t = Tile(turn, base, j, LAG_U)
                if t.live:
                    dve.wait_ge(s_ru, t.n + 1)
                    at_least(dve, s_ul, t.n - 3)
                    dve.tensor_tensor(us[:, t.at % 4], x1s[:, t.slot % 2, TN * t.g:TN * (t.g + 1)], ubank[:, 0:TN],
                                      ALU.mult).then_inc(s_u, 1)
                norm_step(turn, base, j, 3)
                t = Tile(turn, base, j, LAG_Z)
                if t.live:
                    dve.wait_ge(s_z, t.n + 1)
                    dve.bn_stats(zstat[:, t.at, :], zbank[t.at % 2][:, 0:TN]).then_inc(s_bn, 1)
                    if t.at == TURN - 1:
                        dve.wait_ge(s_bn, t.n + 1)
                        own_instruction(dve, s_tally)
                        dve.bn_aggr(zmv[:, :], zstat[:, :, :].rearrange("p n k -> p (n k)")).then_inc(s_agg, 1)
                        dve.wait_ge(s_agg, 2 * t.turn + 1)
                        dst = zturn[:, bass.ds(t.turn, 1), 1:3].rearrange("p o k -> p (o k)")
                        dve.tensor_copy(dst, zmv[:, :]).then_inc(s_agg, 1)

            ticks(dve, tick)

            count = [0]

            def step(ins):
                count[0] += 1
                ins.then_inc(s_bnv, 1)
                dve.wait_ge(s_bnv, count[0])

            def v(i):
                return vec[:, i:i + 1]

            dve.wait_ge(s_agg, 2 * TURNS)
            step(dve.bn_aggr(zmv[:, :], zturn[:, :, :].rearrange("p n k -> p (n k)")))
            step(dve.tensor_scalar(v(0), zmv[:, 1:2], EPS_BN, None, ALU.add))
            dve.sem_inc(s_passa, 1)
            dve.wait_ge(s_bsd, 1)
            step(dve.reciprocal(v(2), v(1)))
            step(dve.tensor_tensor(v(3), v(2), v(2), ALU.mult))
            step(dve.tensor_tensor(v(3), v(3), v(0), ALU.mult))
            step(dve.tensor_scalar(v(3), v(3), -0.5, 1.5, ALU.mult, ALU.add))
            step(dve.tensor_tensor(v(4), v(2), v(3), ALU.mult))
            dve.wait_ge(s_param, 64)
            step(dve.tensor_tensor(v(5), v(4), gam[:, :], ALU.mult))
            step(dve.tensor_tensor(v(6), v(5), zmv[:, 0:1], ALU.mult))
            step(dve.tensor_tensor(v(7), bet[:, :], v(6), ALU.subtract))
            step(dve.tensor_scalar(w_t[:, :], ident[:, :], v(5), None, ALU.mult))
            step(dve.tensor_copy(b3b[:, 0:1], v(7)))
            step(dve.tensor_copy(b3f[:, 0:1], b3b[:, 0:1]))
            step(dve.tensor_tensor(v(8), v(7), b3f[:, 0:1], ALU.subtract))
            step(dve.tensor_copy(b3b[:, 1:2], v(8)))
            step(dve.tensor_copy(b3f[:, 1:2], b3b[:, 1:2]))
            step(dve.tensor_tensor(v(9), v(8), b3f[:, 1:2], ALU.subtract))
            step(dve.tensor_copy(b3b[:, 2:3], v(9)))
            step(dve.tensor_copy(b3f[:, 2:3], b3b[:, 2:3]))
            dve.sem_inc(s_bnok, 1)
            dve.wait_ge(s_bnp, 2)
            dve.tensor_copy(a_t[:, :], banks[4][:, 0:128]).then_inc(s_bnok, 1)
            dve.tensor_copy(b3t[:, :], banks[5][0:3, 0:128]).then_inc(s_bnok, 1)

            def scale(m, k, slot, n):
                dve.wait_ge(s_rc, n + 1)
                at_least(dve, s_inj, n - 1)
                dve.tensor_tensor(xr[k][:, :, :].rearrange("p t b -> p b t"),
                                  chunk[:, slot * B:(slot + 1) * B, bass.ds(m * BT, BT)],
                                  rcbank[k][:, :].rearrange("p (b t) -> p b t", t=BT), ALU.mult).then_inc(s_xr, 1)

            dve.wait_ge(s_ch[0], 64)
            for k in range(2):
                scale(k, k, 0, k)
            with dve.Fori(1, BPC // 2) as m:
                for k in range(2):
                    scale(m * 2 + k, k, 0, m * 2 + k)
            with dve.Fori(0, (CHUNKS - 1) // RING) as lap:
                for r in range(1, RING + 1):
                    slot = r % RING
                    dve.wait_ge(s_ch[slot], 64 * (lap + r // RING + 1))
                    own_instruction(dve, s_tally)
                    first = dve.snap((lap * RING + r) * BPC)
                    with dve.Fori(0, BPC // 2) as m:
                        for k in range(2):
                            scale(m * 2 + k, k, slot, first + (m * 2 + k))

        @block.tensor
        def _(pe):
            pe.wait_ge(s_param, 64)
            pe.wait_ge(s_const, 1)
            pe.wait_ge(s_fixed, 11)
            pe.transpose(banks[2][:, 0:128], w_nat[:, :], ident[:, :]).then_inc(s_prep, 1)
            pe.transpose(banks[3][:, 0:128], v_nat[:, :], ident[:, :]).then_inc(s_prep, 1)
            pe.wait_ge(s_prepc, 1)
            pe.matmul(banks[4][:, 0:128], center[:, :], w_t[:, :], start=True, stop=True).then_inc(s_prep, 1)
            pe.matmul(banks[5][:, 0:128], w_t[:, :], center[:, :], start=True, stop=True).then_inc(s_prep, 1)

            def tick(turn, base, j):
                if isinstance(turn, int) and turn == 0 and j == LAG_NORM - 1:
                    pe.wait_ge(s_band, 16 * HALF)
                    pe.matmul(banks[6][:, 0:TAPS * 128], center[:, :], cw[:, :, :].rearrange("p l k -> p (l k)"),
                              start=True, stop=True).then_inc(s_prep, 1)
                if isinstance(turn, int) and turn == 0 and j == LAG_CONV:
                    pe.wait_ge(s_prepc, 7)
                t = Tile(turn, base, j, LAG_NORM)
                if t.live:
                    if t.g == 0:
                        pe.wait_ge(s_r3a, t.image + 1)
                    at_least(pe, s_xn, t.n)
                    par = t.slot % 2
                    pe.matmul(rbank[:, 0:W], pick[:, (t.g - 1) % TPI, :], r3a[par][:, TN - W:TN],
                              start=True, stop=True)
                    pe.matmul(rbank[:, W:TN], pick[:, t.g, :], r3a[par][:, 0:TN - W],
                              start=True, stop=True).then_inc(s_rb, 1)
                t = Tile(turn, base, j, LAG_CONV)
                if t.live:
                    pe.wait_ge(s_xl, t.n + 1)
                    at_least(pe, s_x1, t.n - 1)
                    o, high, low = cbank[t.at % 2], xh[:, t.at % 4], xl[:, t.at % 4]
                    for tap in (1, 0, 2):
                        width = W - 1 if tap == 2 else W
                        dst = o[:, 0:TN].rearrange("p (r w) -> p r w", w=W)[:, :, 0:width]
                        for i, (w, v) in enumerate([(cw_h, high), (cw_h, low), (cw_l, high)]):
                            last = pe.matmul(dst, w[:, tap, :], v[:, :, tap:tap + width],
                                             start=(tap == 1 and i == 0), stop=(tap == 2 and i == 2))
                    last.then_inc(s_conv, 1)
                t = Tile(turn, base, j, LAG_U)
                if t.live:
                    if t.g == 0:
                        pe.wait_ge(s_r3b, t.image + 1)
                    at_least(pe, s_u, t.n)
                    pe.matmul(ubank[:, 0:TN], pick[:, t.g, :], r3b[t.slot % 2][:, :],
                              start=True, stop=True).then_inc(s_ru, 1)
                t = Tile(turn, base, j, LAG_Z)
                if t.live:
                    pe.wait_ge(s_ul, t.n + 1)
                    at_least(pe, s_bn, t.n - 1)
                    high, low = uh[:, t.at % 4], ul[:, t.at % 4]
                    for i, (w, v) in enumerate([(wc_h, high), (wc_h, low), (wc_l, high)]):
                        last = pe.matmul(zbank[t.at % 2][:, 0:TN], w[:, :], v, start=(i == 0), stop=(i == 2))
                    last.then_inc(s_z, 1)
                t, t1 = Tile(turn, base, j, 0), Tile(turn, base, j, LAG_SUMS1)
                sel = row_mean[:, 31 - j % TPI:63 - j % TPI]
                first, last = j % TPI == 0, j % TPI == TPI - 1
                bank = sums[t.slot % 2]
                if (t.live or t1.live) and first:
                    at_least(pe, s_sub, turn * SLOTS + j // TPI - 1)
                if t.live:
                    pe.wait_ge(s_sq, t.n + 1)
                if t1.live:
                    pe.wait_ge(s_sq1, t1.n + 1)
                if t.live:
                    pe.matmul(bank[0:32, 0:TN], sel,
                              xs[:, t.slot, ROWS * t.g:ROWS * (t.g + 1), :].rearrange("p h w -> p (h w)"),
                              start=first, stop=last)
                    pe.matmul(bank[64:96, 0:TN], sel, xsq[:, t.at % 2], start=first, stop=last).then_inc(s_sum0, 1)
                if t1.live:
                    pe.matmul(bank[32:64, 0:TN], sel, x1s[:, t1.slot % 2, TN * t1.g:TN * (t1.g + 1)],
                              start=first, stop=last)
                    pe.matmul(bank[96:128, 0:TN], sel, x1sq[:, t1.at % 2], start=first,
                              stop=last).then_inc(s_sum1, 1)

            ticks(pe, tick)

            pe.wait_ge(s_bnok, 1)
            pe.matmul(banks[4][:, 0:128], wc_nat[:, :], w_t[:, :], start=True, stop=True).then_inc(s_bnp, 1)
            pe.transpose(banks[5][0:3, 0:128], b3f[:, :], ident[:, :]).then_inc(s_bnp, 1)
            pe.wait_ge(s_bnok, 3)

            def spread(n, k, g):
                at_least(pe, s_xr, n - 1)
                parity, first = g
                pe.matmul(rcbank[k][:, :], ones3[:, 0:128], rg[parity][:, :, BT * first:BT * (first + 1)],
                          start=True, stop=True).then_inc(s_rc, 1)

            def offset(k):
                pe.matmul(pre[k][:, :], b3t[:, :], ones3[:, :], start=True, stop=False, skip_group_check=True)

            def project(k, t):
                ins = pe.matmul(pre[k][:, B * t:B * (t + 1)], a_t[:, :], xr[k][:, t, :], start=False,
                                stop=False, skip_group_check=True)
                if t == BT - 1:
                    ins.then_inc(s_inj, 1)

            def recur(k, t):
                y = ys[k][:, t - 1, :] if t else ys[1 - k][:, BT - 1, :]
                pe.matmul(pre[k][:, B * t:B * (t + 1)], v_t[:, :], y, start=False, stop=True,
                          skip_group_check=True).then_inc(s_pre, 1)

            def group_of(i):
                return i // BPG % 2, i % BPG

            pe.wait_ge(s_rg[0], 16)
            spread(0, 0, group_of(0))
            spread(1, 1, group_of(1))
            offset(0)
            pe.wait_ge(s_xr, 1)
            for t in range(BT):
                project(0, t)

            def turn_of_blocks(q, base, last):
                for i in range(PAIR):
                    n = base + i
                    k = i % 2
                    for t in range(BT):
                        at_least(pe, s_y, n * BT + t)
                        recur(k, t)
                        if t == 1 and not (last and i + 2 >= PAIR):
                            if (i + 2) % BPG == 0:
                                pe.wait_ge(s_rg[(i + 2) // BPG % 2], (q + (2 if i + 2 == PAIR else 1)) * 16)
                            spread(n + 2, k, group_of(i + 2))
                        if not (last and i + 1 >= PAIR):
                            if t == 0:
                                offset(1 - k)
                                pe.wait_ge(s_xr, n + 2)
                            project(1 - k, t)

            turn_of_blocks(0, 0, False)
            with pe.Fori(1, BLOCKS // PAIR - 1) as q:
                turn_of_blocks(q, pe.snap(q * PAIR), False)
            turn_of_blocks(BLOCKS // PAIR - 1, BLOCKS - PAIR, True)


def n_norm_parity(j):
    return (j // TPI - 1) % 2


_INS = ['x', 'L0_conv_W', 'L0_ffn_W', 'L0_ffn_V', 'L0_ffn_gamma', 'L0_ffn_beta']


def kernel(**inputs):
    import numpy as np
    import concourse.bacc as bacc
    from concourse.bass_utils import run_bass_kernel_spmd

    nc = bacc.Bacc("TRN2", target_bir_lowering=False, num_devices=1)
    arrays, args = {}, []
    for name in _INS:
        a = np.ascontiguousarray(inputs[name])
        arrays[f"in_{name}"] = a
        args.append(nc.dram_tensor(f"in_{name}", a.shape, mybir.dt.from_np(a.dtype), kind="ExternalInput").ap())
    out = nc.dram_tensor("out_x", (B, C, H, W), F32, kind="ExternalOutput").ap()
    metaformer_layer(nc, *args, out)
    r = run_bass_kernel_spmd(nc, [arrays], core_ids=[0])
    return r.results[0]["out_x"]
```

```python
from contextlib import ExitStack

import concourse.bass as bass
from concourse import mybir

ALU = mybir.AluOpType
ACT = mybir.ActivationFunctionType
F32 = mybir.dt.float32
BF16 = mybir.dt.bfloat16
F16 = mybir.dt.float16

B, C, H, W = 128, 128, 56, 56
TOK = H * W
HALF = C // 2
TAPS = 3
ROWS = 8
TN = ROWS * W
TPI = TOK // TN
TILES = B * TPI
SLOTS = 4
TURN = SLOTS * TPI
TURNS = TILES // TURN
PADW = W + 2
EPS_C, EPS_T, EPS_BN = 1e-6, 1e-5, 1e-5

LAG_FOLD = 10
LAG_NORM = 11
LAG_HIGH = 11
LAG_LOW = 12
LAG_CONV = 13
LAG_SUMS1 = 14
LAG_U = 25
LAG_UHIGH = 25
LAG_ULOW = 26
LAG_Z = 27
LAST = 27
FILL = 2
NSTEPS = 7
NORMS = B + LAG_SUMS1 // TPI

CH = 112
CHUNKS = TOK // CH
RING = 3
GRP = 28
BT = 4
BLOCKS = TOK // BT
BPG = GRP // BT
BPC = CH // BT
PAIR = 2 * BPG
CHAINS = 2
HB = B // CHAINS
HPAD = 96


def at_least(eng, sem, value):
    if not isinstance(value, int) or value > 0:
        eng.wait_ge(sem, value)


def own_instruction(eng, sem):
    eng.sem_inc(sem, 1)


class Tile:

    def __init__(self, turn, base, j, lag):
        self.n = base + (j - lag)
        self.live = not isinstance(turn, int) or 0 <= self.n < TILES
        at = (j - lag) % TURN
        self.turn = turn if j >= lag else turn - 1
        self.at = at
        self.slot = at // TPI
        self.g = at % TPI
        self.image = self.turn * SLOTS + self.slot


def norm_round(turn, j):
    n = turn * SLOTS + j // TPI
    return None if isinstance(turn, int) and not 0 < n <= NORMS else n, j % TPI


def ticks(eng, tick):
    for j in range(FILL * TURN):
        tick(j // TURN, j // TURN * TURN, j % TURN)
    with eng.Fori(FILL, TURNS) as turn:
        base = eng.snap(turn * TURN)
        for j in range(TURN):
            tick(turn, base, j)
    for j in range(LAST):
        tick(TURNS, TILES, j)


def metaformer_layer(nc, x, conv_w, ffn_w, ffn_v, gamma, beta, out):
    x1_dram = nc.dram_tensor("x1_dram", (CHUNKS, C, B, CH), F32).ap()
    rstd_dram = nc.dram_tensor("rstd_dram", (3, B, TOK), BF16).ap()
    band_dram = nc.dram_tensor("band_dram", (HALF + 4, TAPS, 128), F32).ap()
    row = TAPS * 128
    band_weights = bass.AP(band_dram.tensor, 0, [[2 * row + 4, HALF // 2], [row, 2 * TAPS], [128, TAPS], [1, 4]])
    x_tok = x.rearrange("b c h w -> b c (h w)")
    out_tok = out.rearrange("b c h w -> c b (h w)")

    with ExitStack() as ctx:
        def sb(name, shape, dt=F32):
            return ctx.enter_context(nc.sbuf_tensor(name, shape, dt))

        def sem(name):
            return ctx.enter_context(nc.semaphore(name))

        arena = sb("arena", [128, RING * B * CH])
        taken = [0]

        def carve(size):
            a = arena[:, taken[0]:taken[0] + size]
            taken[0] += size
            return a

        xs = carve(SLOTS * TOK).rearrange("p (s h w) -> p s h w", s=SLOTS, w=W)
        x1s = carve(2 * TOK).rearrange("p (s t) -> p s t", s=2)
        xsq = carve(2 * TN).rearrange("p (s t) -> p s t", s=2)
        x1sq = carve(2 * TN).rearrange("p (s t) -> p s t", s=2)
        x_up = carve(2 * TOK).rearrange("p (s h w) -> p s h w", s=2, w=W)
        folded = carve(4 * TN).rearrange("p (s r w) -> p s r w", s=4, w=W)
        xn = carve(4 * ROWS * PADW).rearrange("p (s r w) -> p s r w", s=4, w=PADW)
        us = carve(4 * TN).rearrange("p (s t) -> p s t", s=4)
        zstat = carve(TURN * 6).rearrange("p (n k) -> p n k", k=6)
        zturn = carve(TURNS * 3).rearrange("p (n k) -> p n k", k=3)
        msq = carve(TN)
        var = carve(TN)
        ln = carve(TN)
        rs = carve(TN)
        nt = carve(TN)
        rd = carve(TN)
        cw = carve(TAPS * 128).rearrange("p (l k) -> p l k", l=TAPS)

        def halves(size):
            return carve(size // 2).bitcast(F16)

        xhl = halves(4 * ROWS * PADW).rearrange("p (s r w) -> p s r w", s=4, w=PADW)
        uh = halves(4 * TN).rearrange("p (s t) -> p s t", s=4)
        ul = halves(4 * TN).rearrange("p (s t) -> p s t", s=4)
        chunk = arena[:, :].rearrange("p (s t) -> p s t", t=CH)

        part = [sb(f"part{i}", [64, TN], BF16) for i in range(3)]
        r3a = [sb(f"r3a{i}", [96, TN], BF16) for i in range(2)]
        r3b = [sb(f"r3b{i}", [96, TN], BF16) for i in range(2)]
        cw_h = sb("cw_h", [128, TAPS, 128], F16)
        cw_l = sb("cw_l", [128, TAPS, 128], F16)
        wc_h = sb("wc_h", [128, 128], F16)
        wc_l = sb("wc_l", [128, 128], F16)
        center = sb("center", [128, 128])
        ident = sb("ident", [128, 128])
        w_nat = sb("w_nat", [128, 128])
        w_t = sb("w_t", [128, 128])
        wc_nat = sb("wc_nat", [128, 128])
        v_nat = sb("v_nat", [128, 128])
        v_t = sb("v_t", [128, 128])
        a_t = sb("a_t", [128, 128])
        pick = sb("pick", [96, TPI, 128], BF16)
        row_mean = sb("row_mean", [128, 63])
        ones3 = sb("ones3", [3, 512], BF16)
        gam = sb("gam", [128, 1])
        bet = sb("bet", [128, 1])
        epsc = sb("epsc", [64, 1])
        vec = sb("vec", [128, 16])
        b3f = sb("b3f", [128, 3])
        b3b = sb("b3b", [128, 3], BF16)
        b3t = sb("b3t", [3, 128], BF16)
        zmv = sb("zmv", [128, 2])
        rg = [sb(f"rg{i}", [3, B, GRP], BF16) for i in range(2)]
        xr = [sb(f"xr{i}", [128, BT, B]) for i in range(2)]
        ys = [sb(f"ys{i}", [128, BT, CHAINS, HPAD]) for i in range(2)]

        banks = [ctx.enter_context(nc.psum_tensor(f"bank{i}", [128, 512], F32)) for i in range(8)]
        sums = banks[0:2]
        rbank, ubank = banks[2], banks[3]
        cbank, zbank = banks[4:6], banks[6:8]
        rcbank, pre = banks[0:2], [banks[2:4], banks[4:6]]

        est, newton, rest = rs[0:64, :], nt[0:64, :], rd[0:64, :]

        s_param = sem("param_loaded")
        s_band = sem("band_loaded")
        s_zero = sem("zeroed")
        s_const = sem("center_ready")
        s_fixed = sem("fixed_values_ready")
        s_prep = sem("prep_product")
        s_prepc = sem("prep_copied")
        s_wready = sem("weights_ready")
        s_x = [sem(f"x_loaded{i}") for i in range(SLOTS)]
        s_xup = [sem(f"x_upper_loaded{i}") for i in range(2)]
        s_fold = sem("folded_ready")
        s_sq = sem("square_ready")
        s_sum0 = sem("tile_summed")
        s_msq = sem("mean_squared")
        s_sub = sem("variance_raw")
        s_var = sem("variance_ready")
        s_ln = sem("log_variance_ready")
        s_est = sem("rstd_estimated")
        s_norm = sem("rstd_step")
        s_r3a = sem("rstd_rows_ready")
        s_r3b = sem("rstd1_rows_ready")
        s_rb = sem("rstd_spread")
        s_xn = sem("normed_ready")
        s_wrap = sem("wrapped_ready")
        s_xh = sem("normed_high_ready")
        s_xl = sem("normed_low_ready")
        s_conv = sem("conv_ready")
        s_x1 = sem("x1_ready")
        s_sq1 = sem("x1_square_ready")
        s_sum1 = sem("x1_tile_summed")
        s_ru = sem("rstd1_spread")
        s_u = sem("u_ready")
        s_uh = sem("u_high_ready")
        s_ul = sem("u_low_ready")
        s_z = sem("z_ready")
        s_bn = sem("z_stats_ready")
        s_agg = sem("turn_stats_ready")
        s_x1st = [sem(f"x1_stored{i}") for i in range(2)]
        s_rst = [sem(f"rstd_stored{i}") for i in range(2)]
        s_bnv = sem("bn_step")
        s_bnp = sem("bn_product")
        s_bsd = sem("bn_deviation")
        s_bnok = sem("bn_weights_ready")
        s_passa = sem("pass_a_over")
        s_tally = sem("waits_over")
        s_ch = [sem(f"chunk_loaded{i}") for i in range(RING)]
        s_rg = [sem(f"group_loaded{i}") for i in range(2)]
        s_rc = sem("rstd_block_spread")
        s_xr = sem("scaled_block_ready")
        s_inj = sem("block_projected")
        s_pre = [sem(f"preactivation_ready{h}") for h in range(CHAINS)]
        s_y = [sem(f"state_ready{h}") for h in range(CHAINS)]
        s_out = sem("block_added")
        s_st = [sem(f"chunk_part_stored{i}") for i in range(4)]

        block = ctx.enter_context(nc.Block())

        @block.sync
        def _(sp):
            sp.dma_start(w_nat[:, :], ffn_w).then_inc(s_param, 16)
            sp.dma_start(v_nat[:, :], ffn_v).then_inc(s_param, 16)
            sp.dma_start(gam[:, :], gamma.rearrange("(h o) -> h o", o=1)).then_inc(s_param, 16)
            sp.dma_start(bet[:, :], beta.rearrange("(h o) -> h o", o=1)).then_inc(s_param, 16)

            def load_image(p):
                sp.dma_start(xs[:, p].rearrange("p h w -> p (h w)"), x_tok[p]).then_inc(s_x[p], 16)

            def load_upper(p, slot):
                sp.dma_start(x_up[0:HALF, slot].rearrange("p h w -> p (h w)"), x_tok[p, HALF:C]).then_inc(s_xup[slot], 16)

            sp.wait_ge(s_zero, 1)
            sp.dma_start(band_dram, cw[0:HALF + 4, :, :]).then_inc(s_band, 16)
            load_image(0)
            load_upper(0, 0)
            sp.wait_ge(s_band, 16)
            sp.dma_start(band_weights, conv_w.rearrange("j i m l k -> j (i m) l k")).then_inc(s_band, 16)
            load_image(1)
            sp.wait_ge(s_band, 32)
            for top in (0, HALF):
                sp.dma_start(cw[top:top + HALF, :, :], band_dram[2:HALF + 2]).then_inc(s_band, 16)
            load_upper(1, 1)
            load_image(2)
            load_image(3)

            def image(turn, at, last):
                done = turn * SLOTS + at + 1
                sp.wait_ge(s_x1, done * TPI)
                if not (last and at >= SLOTS - 2):
                    load_upper(done + 1, at % 2)
                if not last:
                    sp.dma_start(xs[:, at].rearrange("p h w -> p (h w)"),
                                 x_tok[done + (SLOTS - 1)]).then_inc(s_x[at], 16)
                at_image = bass.ds(done - 1, 1)
                sp.dma_start(x1_dram[:, :, at_image, :].rearrange("k c o t -> c (k o) t"),
                             x1s[:, at % 2].rearrange("p (k t) -> p k t", t=CH)).then_inc(s_x1st[at % 2], 16)
                sp.wait_ge(s_r3b, done)
                for q in range(3):
                    sp.dma_start(rstd_dram[q, at_image, :].rearrange("o (g t) -> (o g) t", g=TPI),
                                 r3b[at % 2][32 * q:32 * q + TPI, :]).then_inc(s_rst[at % 2], 16)

            with sp.Fori(0, TURNS - 1) as turn:
                for at in range(SLOTS):
                    image(turn, at, False)
            for at in range(SLOTS):
                image(TURNS - 1, at, True)

            for i in range(2):
                sp.wait_ge(s_x1st[i], 16 * B // 2)
                sp.wait_ge(s_rst[i], 48 * B // 2)
            sp.wait_ge(s_passa, 1)

            def load_group(parity, first):
                sp.dma_start(rg[parity][:, :, :], rstd_dram[:, :, bass.ds(first, GRP)]).then_inc(s_rg[parity], 16)

            QB = B // 4

            def load_part(c, slot, q):
                at = slot * B + q * QB
                sp.dma_start(chunk[:, at:at + QB, :],
                             x1_dram[bass.ds(c, 1), :, q * QB:(q + 1) * QB, :].rearrange("o c b t -> (o c) b t")
                             ).then_inc(s_ch[slot], 16)

            def store_part(c, slot, q):
                at = slot * B + q * QB
                sp.dma_start(out_tok[:, q * QB:(q + 1) * QB, bass.ds(c * CH, CH)],
                             chunk[:, at:at + QB, :]).then_inc(s_st[q], 16)

            load_group(0, 0)
            for q in range(4):
                load_part(0, 0, q)
            load_group(1, GRP)
            for c in range(1, RING):
                for q in range(4):
                    load_part(c, c, q)

            G = BPC // BPG

            def chunk_step(c, slot, groups, store, load):
                prev = (slot + RING - 1) % RING
                for q in range(G):
                    if q < groups:
                        sp.wait_ge(s_rc, (c * G + (q + 1)) * BPG)
                        load_group(q % 2, (c * G + (q + 2)) * GRP)
                    if store:
                        if q == 0:
                            sp.wait_ge(s_out, c * BPC)
                        store_part(c - 1, prev, q)
                    if load and q > 0:
                        sp.wait_ge(s_st[q - 1], c * 16)
                        load_part(c + (RING - 1), prev, q - 1)
                if load:
                    sp.wait_ge(s_st[G - 1], c * 16)
                    load_part(c + (RING - 1), prev, G - 1)

            chunk_step(0, 0, G, False, False)
            with sp.Fori(0, (CHUNKS - 1 - RING) // RING) as lap:
                for k in range(1, RING + 1):
                    chunk_step(lap * RING + k, k % RING, G, True, True)
            first = 1 + (CHUNKS - 1 - RING) // RING * RING
            for c in range(first, CHUNKS):
                chunk_step(c, c % RING, G if c < CHUNKS - 1 else G - 2, True, c + RING - 1 < CHUNKS)
            slot = (CHUNKS - 1) % RING
            for half in range(2):
                sp.wait_ge(s_out, BLOCKS - (1 - half) * BPC // 2)
                t0 = half * CH // 2
                for q in range(4):
                    sp.dma_start(out_tok[:, q * QB:(q + 1) * QB, (CHUNKS - 1) * CH + t0:(CHUNKS - 1) * CH + t0 + CH // 2],
                                 chunk[:, slot * B + q * QB:slot * B + (q + 1) * QB, t0:t0 + CH // 2]
                                 ).then_inc(s_st[q], 16)
            for q in range(4):
                sp.wait_ge(s_st[q], 16 * (CHUNKS + 1))

        @block.gpsimd
        def _(pool):
            pool.memset(cw[:, :, :], 0.0).then_inc(s_zero, 1)
            pool.memset(ident[:, :], 0.0).then_inc(s_zero, 1)
            pool.memset(pick[:, :, :], 0.0).then_inc(s_zero, 1)
            pool.wait_ge(s_zero, 3)
            pool.affine_select(out=ident[:, :], in_=ident[:, :], compare_op=ALU.not_equal, fill=1.0, base=0,
                               pattern=[[-1, 128]], channel_multiplier=1).then_inc(s_zero, 1)
            for q in range(3):
                pool.wait_ge(s_zero, 4 + q)
                v = pick[32 * q:32 * q + 32, :, :]
                pool.affine_select(out=v, in_=v, compare_op=ALU.not_equal, fill=1.0, base=0,
                                   pattern=[[-1, TPI], [0, 128]], channel_multiplier=1).then_inc(s_zero, 1)
            pool.wait_ge(s_zero, 7)
            pool.tensor_scalar(center[:, :], ident[:, :], -1.0 / C, None, ALU.add).then_inc(s_const, 1)

            def tick(turn, base, j):
                n, at = norm_round(turn, j)
                if n is not None and at == 3:
                    pool.wait_ge(s_norm, (n - 1) * NSTEPS + 6)
                    pool.tensor_tensor(part[2][:, :], rest, part[1][:, :], ALU.subtract).then_inc(s_norm, 1)
                t = Tile(turn, base, j, LAG_FOLD)
                if t.live:
                    if t.g == 0:
                        pool.wait_ge(s_x[t.slot], 16 * (t.turn + 1))
                        pool.wait_ge(s_xup[t.slot % 2], 16 * (t.turn * 2 + (t.slot // 2 + 1)))
                    at_least(pool, s_xn, t.n - 3)
                    dst, lower, upper = folded[0:HALF, t.at % 4], xs[0:HALF, t.slot], x_up[0:HALF, t.slot % 2]
                    r0 = ROWS * t.g - 1
                    if t.g == 0:
                        pool.tensor_tensor(dst[:, 0:1, :], lower[:, H - 1:H, :], upper[:, H - 1:H, :], ALU.add)
                        last = pool.tensor_tensor(dst[:, 1:ROWS, :], lower[:, 0:ROWS - 1, :],
                                                  upper[:, 0:ROWS - 1, :], ALU.add)
                    else:
                        last = pool.tensor_tensor(dst, lower[:, r0:r0 + ROWS, :], upper[:, r0:r0 + ROWS, :], ALU.add)
                    last.then_inc(s_fold, 1)
                t = Tile(turn, base, j, LAG_ULOW)
                if t.live:
                    pool.wait_ge(s_uh, t.n + 1)
                    at_least(pool, s_z, t.n - 3)
                    pool.tensor_tensor(ul[:, t.at % 4], us[:, t.at % 4], uh[:, t.at % 4],
                                       ALU.subtract).then_inc(s_ul, 1)
                if n is not None and at == 1:
                    pool.wait_ge(s_norm, (n - 1) * NSTEPS + 1)
                    pool.tensor_tensor(newton, newton, var[0:64, :], ALU.mult).then_inc(s_norm, 1)
                if n is not None and at == 2:
                    pool.wait_ge(s_norm, (n - 1) * NSTEPS + 4)
                    pool.tensor_tensor(rest, newton, part[0][:, :], ALU.subtract).then_inc(s_norm, 1)

            ticks(pool, tick)

            with pool.Fori(0, CHUNKS) as c:
                slot = pool.snap((c % RING) * B)
                with pool.Fori(0, BPC // 2) as m2:
                    for k in range(2):
                        m = m2 * 2 + k
                        n = c * BPC + m
                        for h in range(CHAINS):
                            pool.wait_ge(s_y[h], (n + 1) * BT)
                        v = chunk[:, bass.ds(slot, B), bass.ds(m * BT, BT)].rearrange("p (h b) t -> p h b t", h=CHAINS)
                        pool.tensor_tensor(v, v, ys[k][:, :, :, 0:HB].rearrange("p t h b -> p h b t"),
                                           ALU.add).then_inc(s_out, 1)

        @block.scalar
        def _(act):
            def tick(turn, base, j):
                n, at = norm_round(turn, j)
                if n is not None and at == 3:
                    act.wait_ge(s_norm, (n - 1) * NSTEPS + 5)
                    act.copy(part[1][:, :], rest).then_inc(s_norm, 1)
                t = Tile(turn, base, j, 0)
                n_norm = turn * SLOTS + j // TPI
                norm = j % TPI == 0 and (not isinstance(turn, int) or 0 < n_norm <= NORMS)
                if norm:
                    if not isinstance(turn, int) or n_norm <= B:
                        act.wait_ge(s_sum0, n_norm * TPI)
                    at_least(act, s_sum1, n_norm * TPI - LAG_SUMS1)
                    act.activation(msq[0:64, :], sums[(n_norm_parity(j))][0:64, 0:TN], ACT.Square).then_inc(s_msq, 1)
                if t.live:
                    if t.g == 0:
                        act.wait_ge(s_x[t.slot], 16 * (t.turn + 1))
                    at_least(act, s_sum0, t.n - 1)
                    act.activation(xsq[:, t.at % 2], xs[:, t.slot, ROWS * t.g:ROWS * (t.g + 1), :],
                                   ACT.Square).then_inc(s_sq, 1)
                t = Tile(turn, base, j, LAG_SUMS1)
                if t.live:
                    act.wait_ge(s_x1, t.n + 1)
                    at_least(act, s_sum1, t.n - 1)
                    act.activation(x1sq[:, t.at % 2], x1s[:, t.slot % 2, TN * t.g:TN * (t.g + 1)],
                                   ACT.Square).then_inc(s_sq1, 1)
                if n is not None and at == 2:
                    act.wait_ge(s_norm, (n - 1) * NSTEPS + 3)
                    act.copy(part[0][:, :], newton).then_inc(s_norm, 1)
                w = Tile(turn, base, j, LAG_HIGH)
                if w.live:
                    act.wait_ge(s_xn, w.n + 1)
                    act.copy(xn[0:HALF, w.at % 4, :, 1:2], xn[0:HALF, w.at % 4, :, PADW - 1:PADW]).then_inc(s_wrap, 1)
                if w.live:
                    act.wait_ge(s_wrap, w.n + 1)
                    at_least(act, s_conv, w.n - 3)
                    act.copy(xhl[0:HALF, w.at % 4, :, 1:PADW], xn[0:HALF, w.at % 4, :, 1:PADW]).then_inc(s_xh, 1)
                if norm:
                    act.wait_ge(s_var, n_norm)
                    act.activation(ln[0:64, :], var[0:64, :], ACT.Ln).then_inc(s_ln, 1)
                    act.wait_ge(s_ln, n_norm)
                    act.activation(est, ln[0:64, :], ACT.Exp, scale=-0.5).then_inc(s_est, 1)
                t = Tile(turn, base, j, LAG_UHIGH)
                if t.live:
                    act.wait_ge(s_u, t.n + 1)
                    at_least(act, s_z, t.n - 3)
                    act.copy(uh[:, t.at % 4], us[:, t.at % 4]).then_inc(s_uh, 1)

            act.preload_act_table_set("natural_log_exp_and_others")
            ticks(act, tick)
            act.wait_ge(s_bnv, 2)
            act.activation(vec[:, 1:2], vec[:, 0:1], ACT.Sqrt).then_inc(s_bsd, 1)

            def two_blocks(n0, at0):
                for k in range(2):
                    at_least(act, s_out, n0 + (k - 1))
                    for t in range(BT):
                        for h in range(CHAINS):
                            act.wait_ge(s_pre[h], at0 + (BT * k + t + 1))
                            act.activation(ys[k][:, t, h, 0:HB], pre[h][k][:, HPAD * t:HPAD * t + HB],
                                           ACT.Sigmoid).then_inc(s_y[h], 1)

            two_blocks(0, 0)
            with act.Fori(2, BLOCKS, 2) as n0:
                two_blocks(n0, act.snap(n0 * BT))

        @block.vector
        def _(dve):
            dve.memset(sums[0][:, :], 0.0).then_inc(s_fixed, 1)
            dve.memset(sums[1][:, :], 0.0).then_inc(s_fixed, 1)
            dve.memset(row_mean[:, :], 0.0).then_inc(s_fixed, 1)
            dve.memset(ones3[:, :], 1.0).then_inc(s_fixed, 1)
            dve.memset(xhl[:, :, :, 0:1], 0.0).then_inc(s_fixed, 1)
            dve.memset(zturn[:, :, 0:1], 1.0).then_inc(s_fixed, 1)
            dve.memset(epsc[0:32, :], EPS_C).then_inc(s_fixed, 1)
            dve.memset(epsc[32:64, :], EPS_T).then_inc(s_fixed, 1)
            for y in ys:
                dve.memset(y[:, :, :, :], 0.0).then_inc(s_fixed, 1)
            dve.wait_ge(s_fixed, 10)
            dve.memset(row_mean[:, 31:32], 1.0 / C).then_inc(s_fixed, 1)
            for k, (dst, bank) in enumerate([(w_t, banks[2]), (v_t, banks[3]), (None, None), (wc_nat, banks[5])]):
                dve.wait_ge(s_prep, k + 1)
                if dst is not None:
                    dve.tensor_copy(dst[:, :], bank[:, 0:128]).then_inc(s_prepc, 1)
            dve.tensor_copy(wc_h[:, :], banks[4][:, 0:128]).then_inc(s_prepc, 1)
            dve.wait_ge(s_prepc, 4)
            dve.tensor_tensor(wc_l[:, :], banks[4][:, 0:128], wc_h[:, :], ALU.subtract).then_inc(s_prepc, 1)

            def band_parts():
                flat = banks[6][:, 0:TAPS * 128]
                high, low = (a[:, :, :].rearrange("p l k -> p (l k)") for a in (cw_h, cw_l))
                dve.wait_ge(s_prep, 5)
                dve.tensor_copy(high, flat).then_inc(s_prepc, 1)
                dve.wait_ge(s_prepc, 6)
                dve.tensor_tensor(low, flat, high, ALU.subtract).then_inc(s_prepc, 1)

            def norm_step(turn, base, j, gap):
                n_norm, tick_in = norm_round(turn, j)
                if n_norm is None:
                    return
                at = (tick_in, gap)
                before = (n_norm - 1) * NSTEPS

                if at == (0, 0):
                    dve.wait_ge(s_msq, n_norm)
                    dve.tensor_tensor(var[0:64, :], sums[n_norm_parity(j)][64:128, 0:TN], msq[0:64, :],
                                      ALU.subtract).then_inc(s_sub, 1)
                elif at == (0, 1):
                    dve.wait_ge(s_sub, n_norm)
                    dve.tensor_scalar(var[0:64, :], var[0:64, :], 0.0, epsc[:, 0:1],
                                      ALU.max, ALU.add).then_inc(s_var, 1)
                elif at == (1, 1):
                    dve.wait_ge(s_est, n_norm)
                    dve.scalar_tensor_tensor(out=newton, in0=est, scalar=-0.5, in1=est,
                                             op0=ALU.mult, op1=ALU.mult).then_inc(s_norm, 1)
                elif at == (2, 0):
                    dve.wait_ge(s_norm, before + 2)
                    dve.scalar_tensor_tensor(out=newton, in0=newton, scalar=1.5, in1=est,
                                             op0=ALU.add, op1=ALU.mult).then_inc(s_norm, 1)
                elif at == (3, 2):
                    dve.wait_ge(s_norm, before + NSTEPS)
                    if Tile(turn, base, j - 3 - TPI, 0).live:
                        for k in range(3):
                            last = dve.tensor_copy(r3a[n_norm_parity(j - 3)][32 * k:32 * k + 32, :], part[k][0:32, :])
                        last.then_inc(s_r3a, 1)
                elif at == (4, 0):
                    second = Tile(turn, base, j - 4 - TPI - LAG_SUMS1, 0)
                    par = n_norm_parity(j - 4)
                    if second.live:
                        if not isinstance(turn, int) or second.n >= 2 * TPI:
                            dve.wait_ge(s_rst[par], 48 * (second.turn * 2 + second.slot // 2))
                        for k in range(3):
                            last = dve.tensor_copy(r3b[par][32 * k:32 * k + 32, :], part[k][32:64, :])
                        last.then_inc(s_r3b, 1)

            def tick(turn, base, j):
                if isinstance(turn, int) and turn == 0 and j == LAG_NORM - 1:
                    band_parts()
                norm_step(turn, base, j, 0)
                t = Tile(turn, base, j, LAG_NORM)
                if t.live:
                    dve.wait_ge(s_rb, t.n + 1)
                    dve.wait_ge(s_fold, t.n + 1)
                    at_least(dve, s_xl, t.n - 3)
                    dve.tensor_tensor(xn[0:HALF, t.at % 4, :, 2:PADW], folded[0:HALF, t.at % 4],
                                      rbank[0:HALF, 0:TN].rearrange("p (r w) -> p r w", w=W),
                                      ALU.mult).then_inc(s_xn, 1)
                norm_step(turn, base, j, 1)
                t = Tile(turn, base, j, LAG_LOW)
                if t.live:
                    dve.wait_ge(s_xh, t.n + 1)
                    at_least(dve, s_conv, t.n - 3)
                    dve.tensor_tensor(xhl[HALF:C, t.at % 4, :, 1:PADW], xn[0:HALF, t.at % 4, :, 1:PADW],
                                      xhl[0:HALF, t.at % 4, :, 1:PADW], ALU.subtract).then_inc(s_xl, 1)
                t = Tile(turn, base, j, LAG_CONV)
                if t.live:
                    dve.wait_ge(s_conv, t.n + 1)
                    if t.g == 0 and (not isinstance(turn, int) or t.n >= 2 * TPI):
                        dve.wait_ge(s_x1st[t.slot % 2], 16 * (t.turn * 2 + t.slot // 2))
                    dve.tensor_tensor(x1s[:, t.slot % 2, TN * t.g:TN * (t.g + 1)],
                                      xs[:, t.slot, ROWS * t.g:ROWS * (t.g + 1), :].rearrange("p h w -> p (h w)"),
                                      cbank[t.at % 2][:, 0:TN], ALU.add).then_inc(s_x1, 1)
                norm_step(turn, base, j, 2)
                t = Tile(turn, base, j, LAG_U)
                if t.live:
                    dve.wait_ge(s_ru, t.n + 1)
                    at_least(dve, s_ul, t.n - 3)
                    dve.tensor_tensor(us[:, t.at % 4], x1s[:, t.slot % 2, TN * t.g:TN * (t.g + 1)], ubank[:, 0:TN],
                                      ALU.mult).then_inc(s_u, 1)
                norm_step(turn, base, j, 3)
                t = Tile(turn, base, j, LAG_Z)
                if t.live:
                    dve.wait_ge(s_z, t.n + 1)
                    dve.bn_stats(zstat[:, t.at, :], zbank[t.at % 2][:, 0:TN]).then_inc(s_bn, 1)
                    if t.at == TURN - 1:
                        dve.wait_ge(s_bn, t.n + 1)
                        own_instruction(dve, s_tally)
                        dve.bn_aggr(zmv[:, :], zstat[:, :, :].rearrange("p n k -> p (n k)")).then_inc(s_agg, 1)
                        dve.wait_ge(s_agg, 2 * t.turn + 1)
                        dst = zturn[:, bass.ds(t.turn, 1), 1:3].rearrange("p o k -> p (o k)")
                        dve.tensor_copy(dst, zmv[:, :]).then_inc(s_agg, 1)

            ticks(dve, tick)

            count = [0]

            def step(ins):
                count[0] += 1
                ins.then_inc(s_bnv, 1)
                dve.wait_ge(s_bnv, count[0])

            def v(i):
                return vec[:, i:i + 1]

            dve.wait_ge(s_agg, 2 * TURNS)
            step(dve.bn_aggr(zmv[:, :], zturn[:, :, :].rearrange("p n k -> p (n k)")))
            step(dve.tensor_scalar(v(0), zmv[:, 1:2], EPS_BN, None, ALU.add))
            dve.sem_inc(s_passa, 1)
            dve.wait_ge(s_bsd, 1)
            step(dve.reciprocal(v(2), v(1)))
            step(dve.tensor_tensor(v(3), v(2), v(2), ALU.mult))
            step(dve.tensor_tensor(v(3), v(3), v(0), ALU.mult))
            step(dve.tensor_scalar(v(3), v(3), -0.5, 1.5, ALU.mult, ALU.add))
            step(dve.tensor_tensor(v(4), v(2), v(3), ALU.mult))
            dve.wait_ge(s_param, 64)
            step(dve.tensor_tensor(v(5), v(4), gam[:, :], ALU.mult))
            step(dve.tensor_tensor(v(6), v(5), zmv[:, 0:1], ALU.mult))
            step(dve.tensor_tensor(v(7), bet[:, :], v(6), ALU.subtract))
            step(dve.tensor_scalar(w_t[:, :], ident[:, :], v(5), None, ALU.mult))
            step(dve.tensor_copy(b3b[:, 0:1], v(7)))
            step(dve.tensor_copy(b3f[:, 0:1], b3b[:, 0:1]))
            step(dve.tensor_tensor(v(8), v(7), b3f[:, 0:1], ALU.subtract))
            step(dve.tensor_copy(b3b[:, 1:2], v(8)))
            step(dve.tensor_copy(b3f[:, 1:2], b3b[:, 1:2]))
            step(dve.tensor_tensor(v(9), v(8), b3f[:, 1:2], ALU.subtract))
            step(dve.tensor_copy(b3b[:, 2:3], v(9)))
            step(dve.tensor_copy(b3f[:, 2:3], b3b[:, 2:3]))
            dve.sem_inc(s_bnok, 1)
            dve.wait_ge(s_bnp, 2)
            dve.tensor_copy(a_t[:, :], banks[4][:, 0:128]).then_inc(s_bnok, 1)
            dve.tensor_copy(b3t[:, :], banks[5][0:3, 0:128]).then_inc(s_bnok, 1)

            def scale(m, k, slot, n):
                dve.wait_ge(s_rc, n + 1)
                at_least(dve, s_inj, n - 1)
                dve.tensor_tensor(xr[k][:, :, :].rearrange("p t b -> p b t"),
                                  chunk[:, slot * B:(slot + 1) * B, bass.ds(m * BT, BT)],
                                  rcbank[k][:, :].rearrange("p (b t) -> p b t", t=BT), ALU.mult).then_inc(s_xr, 1)

            dve.wait_ge(s_ch[0], 64)
            for k in range(2):
                scale(k, k, 0, k)
            with dve.Fori(1, BPC // 2) as m:
                for k in range(2):
                    scale(m * 2 + k, k, 0, m * 2 + k)
            with dve.Fori(0, (CHUNKS - 1) // RING) as lap:
                for r in range(1, RING + 1):
                    slot = r % RING
                    dve.wait_ge(s_ch[slot], 64 * (lap + r // RING + 1))
                    own_instruction(dve, s_tally)
                    first = dve.snap((lap * RING + r) * BPC)
                    with dve.Fori(0, BPC // 2) as m:
                        for k in range(2):
                            scale(m * 2 + k, k, slot, first + (m * 2 + k))

        @block.tensor
        def _(pe):
            pe.wait_ge(s_param, 64)
            pe.wait_ge(s_const, 1)
            pe.wait_ge(s_fixed, 11)
            pe.transpose(banks[2][:, 0:128], w_nat[:, :], ident[:, :]).then_inc(s_prep, 1)
            pe.transpose(banks[3][:, 0:128], v_nat[:, :], ident[:, :]).then_inc(s_prep, 1)
            pe.wait_ge(s_prepc, 1)
            pe.matmul(banks[4][:, 0:128], center[:, :], w_t[:, :], start=True, stop=True).then_inc(s_prep, 1)
            pe.matmul(banks[5][:, 0:128], w_t[:, :], center[:, :], start=True, stop=True).then_inc(s_prep, 1)

            def tick(turn, base, j):
                if isinstance(turn, int) and turn == 0 and j == LAG_NORM - 1:
                    pe.wait_ge(s_band, 64)
                    pe.matmul(banks[6][:, 0:TAPS * 128], center[:, :], cw[:, :, :].rearrange("p l k -> p (l k)"),
                              start=True, stop=True).then_inc(s_prep, 1)
                if isinstance(turn, int) and turn == 0 and j == LAG_CONV:
                    pe.wait_ge(s_prepc, 7)
                t = Tile(turn, base, j, LAG_NORM)
                if t.live:
                    if t.g == 0:
                        pe.wait_ge(s_r3a, t.image + 1)
                    at_least(pe, s_xn, t.n)
                    par = t.slot % 2
                    pe.matmul(rbank[:, 0:W], pick[:, (t.g - 1) % TPI, :], r3a[par][:, TN - W:TN],
                              start=True, stop=True)
                    pe.matmul(rbank[:, W:TN], pick[:, t.g, :], r3a[par][:, 0:TN - W],
                              start=True, stop=True).then_inc(s_rb, 1)
                t = Tile(turn, base, j, LAG_CONV)
                if t.live:
                    pe.wait_ge(s_xl, t.n + 1)
                    at_least(pe, s_x1, t.n - 1)
                    o, parts = cbank[t.at % 2], xhl[:, t.at % 4]
                    for tap in (1, 0, 2):
                        width = W - 1 if tap == 2 else W
                        dst = o[:, 0:TN].rearrange("p (r w) -> p r w", w=W)[:, :, 0:width]
                        for w in (cw_h, cw_l):
                            last = pe.matmul(dst, w[:, tap, :], parts[:, :, tap:tap + width],
                                             start=(tap == 1 and w is cw_h), stop=(tap == 2 and w is cw_l))
                    last.then_inc(s_conv, 1)
                t = Tile(turn, base, j, LAG_U)
                if t.live:
                    if t.g == 0:
                        pe.wait_ge(s_r3b, t.image + 1)
                    at_least(pe, s_u, t.n)
                    pe.matmul(ubank[:, 0:TN], pick[:, t.g, :], r3b[t.slot % 2][:, :],
                              start=True, stop=True).then_inc(s_ru, 1)
                t = Tile(turn, base, j, LAG_Z)
                if t.live:
                    pe.wait_ge(s_ul, t.n + 1)
                    at_least(pe, s_bn, t.n - 1)
                    high, low = uh[:, t.at % 4], ul[:, t.at % 4]
                    for i, (w, v) in enumerate([(wc_h, high), (wc_h, low), (wc_l, high)]):
                        last = pe.matmul(zbank[t.at % 2][:, 0:TN], w[:, :], v, start=(i == 0), stop=(i == 2))
                    last.then_inc(s_z, 1)
                t, t1 = Tile(turn, base, j, 0), Tile(turn, base, j, LAG_SUMS1)
                sel = row_mean[:, 31 - j % TPI:63 - j % TPI]
                first, last = j % TPI == 0, j % TPI == TPI - 1
                bank = sums[t.slot % 2]
                if (t.live or t1.live) and first:
                    at_least(pe, s_sub, turn * SLOTS + j // TPI - 1)
                if t.live:
                    pe.wait_ge(s_sq, t.n + 1)
                if t1.live:
                    pe.wait_ge(s_sq1, t1.n + 1)
                if t.live:
                    pe.matmul(bank[0:32, 0:TN], sel,
                              xs[:, t.slot, ROWS * t.g:ROWS * (t.g + 1), :].rearrange("p h w -> p (h w)"),
                              start=first, stop=last)
                    pe.matmul(bank[64:96, 0:TN], sel, xsq[:, t.at % 2], start=first, stop=last).then_inc(s_sum0, 1)
                if t1.live:
                    pe.matmul(bank[32:64, 0:TN], sel, x1s[:, t1.slot % 2, TN * t1.g:TN * (t1.g + 1)],
                              start=first, stop=last)
                    pe.matmul(bank[96:128, 0:TN], sel, x1sq[:, t1.at % 2], start=first,
                              stop=last).then_inc(s_sum1, 1)

            ticks(pe, tick)

            pe.wait_ge(s_bnok, 1)
            pe.matmul(banks[4][:, 0:128], wc_nat[:, :], w_t[:, :], start=True, stop=True).then_inc(s_bnp, 1)
            pe.transpose(banks[5][0:3, 0:128], b3f[:, :], ident[:, :]).then_inc(s_bnp, 1)
            pe.wait_ge(s_bnok, 3)

            def spread(n, k, g):
                at_least(pe, s_xr, n - 1)
                parity, first = g
                pe.matmul(rcbank[k][:, :], ones3[:, 0:128], rg[parity][:, :, BT * first:BT * (first + 1)],
                          start=True, stop=True).then_inc(s_rc, 1)

            def token_columns(k, h, first, count):
                cols = pre[h][k][:, first * HPAD:(first + count) * HPAD]
                return cols.rearrange("p (t b) -> p t b", b=HPAD)[:, :, 0:HB]

            def offset(k, h):
                pe.matmul(token_columns(k, h, 0, BT), b3t[:, :], ones3[:, 0:BT * HB], start=True, stop=False,
                          skip_group_check=True)

            def project(k, h, two):
                ins = pe.matmul(token_columns(k, h, 2 * two, 2), a_t[:, :],
                                xr[k][:, 2 * two:2 * (two + 1), HB * h:HB * (h + 1)],
                                start=False, stop=False, skip_group_check=True)
                if (h, two) == (CHAINS - 1, 1):
                    ins.then_inc(s_inj, 1)

            def recur(k, h, t):
                y = ys[k][:, t - 1, h, :] if t else ys[1 - k][:, BT - 1, h, :]
                pe.matmul(pre[h][k][:, HPAD * t:HPAD * (t + 1)], v_t[:, :], y, start=False, stop=True,
                          skip_group_check=True).then_inc(s_pre[h], 1)

            def group_of(i):
                return i // BPG % 2, i % BPG

            pe.wait_ge(s_rg[0], 16)
            spread(0, 0, group_of(0))
            spread(1, 1, group_of(1))
            for k in range(2):
                for h in range(CHAINS):
                    pe.matmul(pre[h][k][:, 0:BT * HPAD], b3t[:, :], ones3[:, 0:BT * HPAD], start=True, stop=True)
            pe.wait_ge(s_xr, 1)
            for h in range(CHAINS):
                offset(0, h)
                for two in range(2):
                    project(0, h, two)

            def turn_of_blocks(q, base, last):
                for i in range(PAIR):
                    n = base + i
                    k = i % 2
                    following = not (last and i + 1 >= PAIR)
                    for t in range(BT):
                        for h in range(CHAINS):
                            at_least(pe, s_y[h], n * BT + t)
                            recur(k, h, t)
                            if following and (t, h) == (0, 0):
                                offset(1 - k, 0)
                            if following and (t, h) == (0, 1):
                                pe.wait_ge(s_xr, n + 2)
                                project(1 - k, 0, 0)
                            if (t, h) == (1, 0) and not (last and i + 2 >= PAIR):
                                if (i + 2) % BPG == 0:
                                    pe.wait_ge(s_rg[(i + 2) // BPG % 2], (q + (2 if i + 2 == PAIR else 1)) * 16)
                                spread(n + 2, k, group_of(i + 2))
                            if following and (t, h) == (1, 1):
                                project(1 - k, 0, 1)
                            if following and (t, h) == (2, 0):
                                offset(1 - k, 1)
                            if following and (t, h) == (2, 1):
                                project(1 - k, 1, 0)
                            if following and (t, h) == (3, 1):
                                project(1 - k, 1, 1)

            turn_of_blocks(0, 0, False)
            with pe.Fori(1, BLOCKS // PAIR - 1) as q:
                turn_of_blocks(q, pe.snap(q * PAIR), False)
            turn_of_blocks(BLOCKS // PAIR - 1, BLOCKS - PAIR, True)


def n_norm_parity(j):
    return (j // TPI - 1) % 2


_INS = ['x', 'L0_conv_W', 'L0_ffn_W', 'L0_ffn_V', 'L0_ffn_gamma', 'L0_ffn_beta']


def kernel(**inputs):
    import numpy as np
    import concourse.bacc as bacc
    from concourse.bass_utils import run_bass_kernel_spmd

    nc = bacc.Bacc("TRN2", target_bir_lowering=False, num_devices=1)
    arrays, args = {}, []
    for name in _INS:
        a = np.ascontiguousarray(inputs[name])
        arrays[f"in_{name}"] = a
        args.append(nc.dram_tensor(f"in_{name}", a.shape, mybir.dt.from_np(a.dtype), kind="ExternalInput").ap())
    out = nc.dram_tensor("out_x", (B, C, H, W), F32, kind="ExternalOutput").ap()
    metaformer_layer(nc, *args, out)
    r = run_bass_kernel_spmd(nc, [arrays], core_ids=[0])
    return r.results[0]["out_x"]
```
